# Optimizing a Trainium2 kernel written in Bass

```python
import numpy as np
import jax
import jax.numpy as jnp

def _softmax(x, axis=-1):
    return jax.nn.softmax(x, axis=axis)

def _gelu(x):
    return jax.nn.gelu(x, approximate=True)

def _silu(x):
    return jax.nn.silu(x)

def _sigmoid(x):
    return jax.nn.sigmoid(x)

def _layernorm(x, axis=-1, eps=1e-05):
    m = jnp.mean(x, axis=axis, keepdims=True)
    v = jnp.var(x, axis=axis, keepdims=True)
    return (x - m) / jnp.sqrt(v + eps)

def _scatter_add(tgt, idx, src, axis=0):
    return tgt.at[idx].add(src)

def _segment_sum(src, seg, n):
    return jax.ops.segment_sum(src, seg, n)
kernel_name = 'mk_cond_seq_d2_seqx_r4_3ef755'

def setup_inputs(seed: int=0):
    np.random.seed(seed)
    _w = jnp.asarray

    def _rec_inputs():
        import jax
        import jax.numpy as jnp
        _rk = jax.random.key(seed)
        x = -0.0002928 + 1 * jax.random.normal(jax.random.fold_in(_rk, 1), (16, 256, 256), jnp.float32)
        _lenS = 256 - jax.random.randint(jax.random.fold_in(_rk, 7), (16,), 0, max(1, 256 // 4) + 1, jnp.int32)
        _lenS2 = 256 - jax.random.randint(jax.random.fold_in(_rk, 8), (16,), 0, max(1, 256 // 4) + 1, jnp.int32)
        itok_B_6_14 = jax.random.randint(jax.random.fold_in(_rk, 11), (16,), 6, 15, jnp.int32)
        itok_B_34_63 = jax.random.randint(jax.random.fold_in(_rk, 13), (16,), 34, 64, jnp.int32)
        fside_Bx16xSxS_0 = -1.47943e-05 + 1.00017 * jax.random.normal(jax.random.fold_in(_rk, 14), (16, 16, 256, 256), jnp.float32)
        _validS = jnp.arange(256)[None, :] < _lenS[:, None]
        _validS2 = jnp.arange(256)[None, :] < _lenS2[:, None]
        _causal = jnp.tril(jnp.ones((256, 256), dtype=bool))
        mask_Bx1xSxS_bk0 = jnp.logical_not(jnp.broadcast_to(_validS[:, None, None, :], (16, 1, 256, 256)))
        return (x, itok_B_6_14, itok_B_34_63, fside_Bx16xSxS_0, mask_Bx1xSxS_bk0)
    x, itok_B_6_14, itok_B_34_63, fside_Bx16xSxS_0, mask_Bx1xSxS_bk0 = _rec_inputs()

    def _L0_cond_setup():
        import jax, jax.numpy as jnp
        import numpy as np
        D = 256
        E = 8
        FF = 1024
        TOPK = 2
        S = 32
        SE = 64
        SH = 128
        B, T = (2, 512)

        def _forward(x, subject_ids, ln_g, ln_b, subj_emb, hyp_w1, hyp_b1, hyp_w2, hyp_b2, sty_w1, sty_b1, sty_w2, sty_b2, router_w, exp_w1, exp_b1, exp_w2, exp_b2):
            mu = x.mean(-1, keepdims=True)
            var = x.var(-1, keepdims=True)
            h = (x - mu) * jax.lax.rsqrt(var + 1e-05) * ln_g + ln_b
            m_t = h.mean(1, keepdims=True)
            v_t = h.var(1, keepdims=True)
            h_norm = (h - m_t) * jax.lax.rsqrt(v_t + 1e-08)
            se = subj_emb[subject_ids]
            hyp = jax.nn.relu(se @ hyp_w1 + hyp_b1) @ hyp_w2 + hyp_b2
            sty = jax.nn.relu(hyp @ sty_w1 + sty_b1) @ sty_w2 + sty_b2
            gamma, beta = jnp.split(sty, 2, axis=-1)
            gamma = jax.nn.softplus(gamma) + 1e-08
            h = h_norm * gamma[:, None, :] + beta[:, None, :]
            h_flat = h.reshape(-1, D)
            probs = jax.nn.softmax(h_flat @ router_w, axis=-1)
            gates, idx = jax.lax.top_k(probs, TOPK)
            gates = gates / gates.sum(-1, keepdims=True)
            N = h_flat.shape[0]
            combine = jnp.zeros((N, E), h_flat.dtype).at[jnp.arange(N)[:, None], idx].add(gates)
            hid = jax.nn.relu(jnp.einsum('nd,edf->nef', h_flat, exp_w1) + exp_b1)
            eout = jnp.einsum('nef,efd->ned', hid, exp_w2) + exp_b2
            y = jnp.einsum('ned,ne->nd', eout, combine)
            return x + y.reshape(x.shape)
        key = jax.random.key(seed)
        ks = jax.random.split(key, 16)
        n = lambda k, sh, s=0.02: jax.random.normal(k, sh, dtype=jnp.float32) * s
        return {'x': jax.random.normal(ks[0], (B, T, D), dtype=jnp.float32), 'subject_ids': jax.random.randint(ks[1], (B,), 0, S), 'ln_g': jnp.ones((D,), jnp.float32), 'ln_b': jnp.zeros((D,), jnp.float32), 'subj_emb': n(ks[2], (S, SE)), 'hyp_w1': n(ks[3], (SE, SH), 1.0 / np.sqrt(SE)), 'hyp_b1': jnp.zeros((SH,), jnp.float32), 'hyp_w2': n(ks[4], (SH, SH), 1.0 / np.sqrt(SH)), 'hyp_b2': jnp.zeros((SH,), jnp.float32), 'sty_w1': n(ks[5], (SH, SH // 2), 1.0 / np.sqrt(SH)), 'sty_b1': jnp.zeros((SH // 2,), jnp.float32), 'sty_w2': n(ks[6], (SH // 2, 2 * D), 1.0 / np.sqrt(SH // 2)), 'sty_b2': jnp.zeros((2 * D,), jnp.float32), 'router_w': n(ks[7], (D, E), 1.0 / np.sqrt(D)), 'exp_w1': n(ks[8], (E, D, FF), 1.0 / np.sqrt(D)), 'exp_b1': jnp.zeros((E, FF), jnp.float32), 'exp_w2': n(ks[9], (E, FF, D), 1.0 / np.sqrt(FF)), 'exp_b2': jnp.zeros((E, D), jnp.float32)}
    _L0_cond_all = _L0_cond_setup()
    _L0_cond_in = {k: v for k, v in _L0_cond_all.items() if k in ('ln_g', 'ln_b', 'subj_emb', 'hyp_w1', 'hyp_b1', 'hyp_w2', 'hyp_b2', 'sty_w1', 'sty_b1', 'sty_w2', 'sty_b2', 'router_w', 'exp_w1', 'exp_b1', 'exp_w2', 'exp_b2')}
    del _L0_cond_all

    def _L1_cond_setup():
        import jax, jax.numpy as jnp
        import numpy as np
        import math
        D_MODEL = 256
        N_HEAD = 16
        HEAD_DIM = D_MODEL // N_HEAD
        D_FF = 1024
        NUM_STEPS = 100.0
        RESCALE = 4000.0
        EPS = 1e-05

        def _sin_emb(t):
            half = D_MODEL // 2
            x = t.astype(jnp.float32) / NUM_STEPS * RESCALE
            freqs = jnp.exp(jnp.arange(half, dtype=jnp.float32) * (-math.log(10000.0) / (half - 1)))
            e = x[:, None] * freqs[None, :]
            return jnp.concatenate([jnp.sin(e), jnp.cos(e)], axis=-1)

        def _ln(x):
            m = jnp.mean(x, axis=-1, keepdims=True)
            v = jnp.var(x, axis=-1, keepdims=True)
            return (x - m) / jnp.sqrt(v + EPS)

        def _gelu2(x):
            return x * jax.nn.sigmoid(1.702 * x)
        key = jax.random.key(seed)
        ks = jax.random.split(key, 24)
        B, S, D, F = (4, 128, D_MODEL, D_FF)
        std = 0.02
        inp = {'src': jax.random.normal(ks[0], (B, S, D), dtype=jnp.float32), 'src_mask': jax.random.randint(ks[1], (B, 1, S, S), 0, 2).astype(bool), 'timestep': jax.random.randint(ks[2], (B,), 0, 100, dtype=jnp.int32), 'attention_bias': jax.random.normal(ks[3], (B, N_HEAD, S, S), dtype=jnp.float32), 'W_ada': jax.random.normal(ks[4], (D, 2 * D), dtype=jnp.float32) * std, 'b_ada': jnp.zeros((2 * D,), dtype=jnp.float32), 'Wq': jax.random.normal(ks[5], (D, D), dtype=jnp.float32) * std, 'bq': jnp.zeros((D,), dtype=jnp.float32), 'Wk': jax.random.normal(ks[6], (D, D), dtype=jnp.float32) * std, 'bk': jnp.zeros((D,), dtype=jnp.float32), 'Wv': jax.random.normal(ks[7], (D, D), dtype=jnp.float32) * std, 'bv': jnp.zeros((D,), dtype=jnp.float32), 'Wo': jax.random.normal(ks[8], (D, D), dtype=jnp.float32) * std, 'bo': jnp.zeros((D,), dtype=jnp.float32), 'W1': jax.random.normal(ks[9], (D, F), dtype=jnp.float32) * std, 'b1': jnp.zeros((F,), dtype=jnp.float32), 'W2': jax.random.normal(ks[10], (F, D), dtype=jnp.float32) * std, 'b2': jnp.zeros((D,), dtype=jnp.float32), 'g2': jnp.ones((D,), dtype=jnp.float32), 'beta2': jnp.zeros((D,), dtype=jnp.float32)}
        return inp
    _L1_cond_all = _L1_cond_setup()
    _L1_cond_in = {k: v for k, v in _L1_cond_all.items() if k in ('W_ada', 'b_ada', 'Wq', 'bq', 'Wk', 'bk', 'Wv', 'bv', 'Wo', 'bo', 'W1', 'b1', 'W2', 'b2', 'g2', 'beta2')}
    del _L1_cond_all
    return {'x': x, 'itok_B_6_14': itok_B_6_14, 'itok_B_34_63': itok_B_34_63, 'fside_Bx16xSxS_0': fside_Bx16xSxS_0, 'mask_Bx1xSxS_bk0': mask_Bx1xSxS_bk0, 'L0_cond_ln_g': _L0_cond_in['ln_g'], 'L0_cond_ln_b': _L0_cond_in['ln_b'], 'L0_cond_subj_emb': _L0_cond_in['subj_emb'], 'L0_cond_hyp_w1': _L0_cond_in['hyp_w1'], 'L0_cond_hyp_b1': _L0_cond_in['hyp_b1'], 'L0_cond_hyp_w2': _L0_cond_in['hyp_w2'], 'L0_cond_hyp_b2': _L0_cond_in['hyp_b2'], 'L0_cond_sty_w1': _L0_cond_in['sty_w1'], 'L0_cond_sty_b1': _L0_cond_in['sty_b1'], 'L0_cond_sty_w2': _L0_cond_in['sty_w2'], 'L0_cond_sty_b2': _L0_cond_in['sty_b2'], 'L0_cond_router_w': _L0_cond_in['router_w'], 'L0_cond_exp_w1': _L0_cond_in['exp_w1'], 'L0_cond_exp_b1': _L0_cond_in['exp_b1'], 'L0_cond_exp_w2': _L0_cond_in['exp_w2'], 'L0_cond_exp_b2': _L0_cond_in['exp_b2'], 'L1_cond_W_ada': _L1_cond_in['W_ada'], 'L1_cond_b_ada': _L1_cond_in['b_ada'], 'L1_cond_Wq': _L1_cond_in['Wq'], 'L1_cond_bq': _L1_cond_in['bq'], 'L1_cond_Wk': _L1_cond_in['Wk'], 'L1_cond_bk': _L1_cond_in['bk'], 'L1_cond_Wv': _L1_cond_in['Wv'], 'L1_cond_bv': _L1_cond_in['bv'], 'L1_cond_Wo': _L1_cond_in['Wo'], 'L1_cond_bo': _L1_cond_in['bo'], 'L1_cond_W1': _L1_cond_in['W1'], 'L1_cond_b1': _L1_cond_in['b1'], 'L1_cond_W2': _L1_cond_in['W2'], 'L1_cond_b2': _L1_cond_in['b2'], 'L1_cond_g2': _L1_cond_in['g2'], 'L1_cond_beta2': _L1_cond_in['beta2']}

def reference(x, itok_B_6_14, itok_B_34_63, fside_Bx16xSxS_0, mask_Bx1xSxS_bk0, L0_cond_ln_g, L0_cond_ln_b, L0_cond_subj_emb, L0_cond_hyp_w1, L0_cond_hyp_b1, L0_cond_hyp_w2, L0_cond_hyp_b2, L0_cond_sty_w1, L0_cond_sty_b1, L0_cond_sty_w2, L0_cond_sty_b2, L0_cond_router_w, L0_cond_exp_w1, L0_cond_exp_b1, L0_cond_exp_w2, L0_cond_exp_b2, L1_cond_W_ada, L1_cond_b_ada, L1_cond_Wq, L1_cond_bq, L1_cond_Wk, L1_cond_bk, L1_cond_Wv, L1_cond_bv, L1_cond_Wo, L1_cond_bo, L1_cond_W1, L1_cond_b1, L1_cond_W2, L1_cond_b2, L1_cond_g2, L1_cond_beta2):
    import jax
    import jax.numpy as jnp

    def _L0_cond_ref(x, subject_ids, ln_g, ln_b, subj_emb, hyp_w1, hyp_b1, hyp_w2, hyp_b2, sty_w1, sty_b1, sty_w2, sty_b2, router_w, exp_w1, exp_b1, exp_w2, exp_b2):
        import jax, jax.numpy as jnp
        import numpy as np
        D = 256
        E = 8
        FF = 1024
        TOPK = 2
        S = 32
        SE = 64
        SH = 128
        B, T = (2, 512)

        def _forward(x, subject_ids, ln_g, ln_b, subj_emb, hyp_w1, hyp_b1, hyp_w2, hyp_b2, sty_w1, sty_b1, sty_w2, sty_b2, router_w, exp_w1, exp_b1, exp_w2, exp_b2):
            mu = x.mean(-1, keepdims=True)
            var = x.var(-1, keepdims=True)
            h = (x - mu) * jax.lax.rsqrt(var + 1e-05) * ln_g + ln_b
            m_t = h.mean(1, keepdims=True)
            v_t = h.var(1, keepdims=True)
            h_norm = (h - m_t) * jax.lax.rsqrt(v_t + 1e-08)
            se = subj_emb[subject_ids]
            hyp = jax.nn.relu(se @ hyp_w1 + hyp_b1) @ hyp_w2 + hyp_b2
            sty = jax.nn.relu(hyp @ sty_w1 + sty_b1) @ sty_w2 + sty_b2
            gamma, beta = jnp.split(sty, 2, axis=-1)
            gamma = jax.nn.softplus(gamma) + 1e-08
            h = h_norm * gamma[:, None, :] + beta[:, None, :]
            h_flat = h.reshape(-1, D)
            probs = jax.nn.softmax(h_flat @ router_w, axis=-1)
            gates, idx = jax.lax.top_k(probs, TOPK)
            gates = gates / gates.sum(-1, keepdims=True)
            N = h_flat.shape[0]
            combine = jnp.zeros((N, E), h_flat.dtype).at[jnp.arange(N)[:, None], idx].add(gates)
            hid = jax.nn.relu(jnp.einsum('nd,edf->nef', h_flat, exp_w1) + exp_b1)
            eout = jnp.einsum('nef,efd->ned', hid, exp_w2) + exp_b2
            y = jnp.einsum('ned,ne->nd', eout, combine)
            return x + y.reshape(x.shape)
        return _forward(x, subject_ids, ln_g, ln_b, subj_emb, hyp_w1, hyp_b1, hyp_w2, hyp_b2, sty_w1, sty_b1, sty_w2, sty_b2, router_w, exp_w1, exp_b1, exp_w2, exp_b2)

    def _L1_cond_ref(src, src_mask, timestep, attention_bias, W_ada, b_ada, Wq, bq, Wk, bk, Wv, bv, Wo, bo, W1, b1, W2, b2, g2, beta2):
        import jax, jax.numpy as jnp
        import numpy as np
        import math
        D_MODEL = 256
        N_HEAD = 16
        HEAD_DIM = D_MODEL // N_HEAD
        D_FF = 1024
        NUM_STEPS = 100.0
        RESCALE = 4000.0
        EPS = 1e-05

        def _sin_emb(t):
            half = D_MODEL // 2
            x = t.astype(jnp.float32) / NUM_STEPS * RESCALE
            freqs = jnp.exp(jnp.arange(half, dtype=jnp.float32) * (-math.log(10000.0) / (half - 1)))
            e = x[:, None] * freqs[None, :]
            return jnp.concatenate([jnp.sin(e), jnp.cos(e)], axis=-1)

        def _ln(x):
            m = jnp.mean(x, axis=-1, keepdims=True)
            v = jnp.var(x, axis=-1, keepdims=True)
            return (x - m) / jnp.sqrt(v + EPS)

        def _gelu2(x):
            return x * jax.nn.sigmoid(1.702 * x)
        B, S, D = src.shape
        emb = jax.nn.silu(_sin_emb(timestep)) @ W_ada + b_ada
        scale, shift = jnp.split(emb[:, None, :], 2, axis=-1)
        x = _ln(src) * (1.0 + scale) + shift
        q = (x @ Wq + bq).reshape(B, S, N_HEAD, HEAD_DIM).transpose(0, 2, 1, 3)
        k = (x @ Wk + bk).reshape(B, S, N_HEAD, HEAD_DIM).transpose(0, 2, 1, 3)
        v = (x @ Wv + bv).reshape(B, S, N_HEAD, HEAD_DIM).transpose(0, 2, 1, 3)
        scores = jnp.einsum('bhqd,bhkd->bhqk', q / math.sqrt(HEAD_DIM), k)
        scores = scores + attention_bias
        scores = jnp.where(src_mask, -jnp.inf, scores.astype(jnp.float32))
        probs = jax.nn.softmax(scores, axis=-1).astype(v.dtype)
        ctx = jnp.einsum('bhqk,bhkd->bhqd', probs, v)
        ctx = ctx.transpose(0, 2, 1, 3).reshape(B, S, D)
        x = x + (ctx @ Wo + bo)
        h = _ln(x) * g2 + beta2
        ff = _gelu2(h @ W1 + b1) @ W2 + b2
        return x + ff
    x = _L0_cond_ref(x, itok_B_6_14, L0_cond_ln_g, L0_cond_ln_b, L0_cond_subj_emb, L0_cond_hyp_w1, L0_cond_hyp_b1, L0_cond_hyp_w2, L0_cond_hyp_b2, L0_cond_sty_w1, L0_cond_sty_b1, L0_cond_sty_w2, L0_cond_sty_b2, L0_cond_router_w, L0_cond_exp_w1, L0_cond_exp_b1, L0_cond_exp_w2, L0_cond_exp_b2)
    x = _L1_cond_ref(x, mask_Bx1xSxS_bk0, itok_B_34_63, fside_Bx16xSxS_0, L1_cond_W_ada, L1_cond_b_ada, L1_cond_Wq, L1_cond_bq, L1_cond_Wk, L1_cond_bk, L1_cond_Wv, L1_cond_bv, L1_cond_Wo, L1_cond_bo, L1_cond_W1, L1_cond_b1, L1_cond_W2, L1_cond_b2, L1_cond_g2, L1_cond_beta2)
    return x

_drawn_inputs = setup_inputs


def setup_inputs(seed=0):
    import zlib

    import numpy as np

    out = dict(_drawn_inputs(seed))
    spreads = {'L0_cond_ln_g': (1.0, 0.6),
     'L0_cond_ln_b': (0.0, 0.8),
     'L0_cond_hyp_b1': (0.0, 0.1),
     'L0_cond_hyp_b2': (0.0, 0.1),
     'L0_cond_sty_b1': (0.0, 0.1),
     'L0_cond_sty_b2': (0.0, 0.1),
     'L0_cond_exp_b1': (0.0, 0.1),
     'L0_cond_exp_b2': (0.0, 0.1),
     'L1_cond_b_ada': (0.0, 0.1),
     'L1_cond_bq': (0.0, 0.8),
     'L1_cond_bk': (0.0, 0.8),
     'L1_cond_bv': (0.0, 0.267),
     'L1_cond_bo': (0.0, 0.1),
     'L1_cond_b1': (0.0, 0.1),
     'L1_cond_b2': (0.0, 0.1),
     'L1_cond_g2': (1.0, 0.6),
     'L1_cond_beta2': (0.0, 0.676)}
    factors = {'fside_Bx16xSxS_0': 6.697, 'L1_cond_Wq': 8.0, 'L1_cond_Wk': 8.0}
    for name, (base, spread) in spreads.items():
        noise = np.random.default_rng([zlib.crc32(name.encode()), seed]).standard_normal(out[name].shape)
        drawn = base * np.exp(spread * noise) if base else spread * noise
        out[name] = jnp.asarray(drawn.astype(out[name].dtype))
    for name, factor in factors.items():
        out[name] = (out[name] * factor).astype(out[name].dtype)
    return out
```

```python
from contextlib import ExitStack

import numpy as np

import concourse.bass as bass
from concourse import mybir

F32 = mybir.dt.float32
F32R = mybir.dt.float32r
I32 = mybir.dt.int32
U32 = mybir.dt.uint32
U8 = mybir.dt.uint8
ALU = mybir.AluOpType
ACT = mybir.ActivationFunctionType
X = mybir.AxisListType.X

P = 128
B, T, D = 16, 256, 256
J = T // P
C = D // P
E, FF = 8, 1024
F = FF // P
K = 2
H, HD = 16, 16
SUBJ, SE, SH = 32, 64, 128
REGION = B * T + P
TILES = (K * B * T - P) // P + E
MAGIC = 8388608.0
MASKED = -3.0e38

LN_G, LN_B, HYP_B1, HYP_B2, STY_B1, STY_B2 = 0, 2, 4, 5, 6, 7
ADA_B, Q_B, K_B, FF_B1, LN2_G, LN2_B = 11, 15, 17, 19, 27, 29
FREQ, PART, VECS = 31, 32, 33
IDENT, BELOW, ONES, SLOT, TILE_NO, REGION_ROW, SPREAD, CONSTS = 0, 128, 256, 384, 392, 464, 472, 728


class Steps:

    def __init__(self, eng, sem, base=0):
        self.eng, self.sem, self.at = eng, sem, base

    def did(self, instruction):
        self.at = self.at + 1
        instruction.then_inc(self.sem, 1)

    def then(self, instruction):
        self.did(instruction)
        self.eng.wait_ge(self.sem, self.at)

    def then_alone(self, instruction):
        self.did(instruction)
        wait_alone(self.eng, self.sem, self.at)


def wait_alone(eng, sem, value):
    if isinstance(value, int):
        eng.wait_ge(sem, value)
    else:
        value = eng.to_reg(value)
        eng.wait_ge(sem, 1)
        eng.wait_ge(sem, value)


def wait_free(eng, sem, value, alone=False):
    if isinstance(value, int):
        if value > 0:
            eng.wait_ge(sem, value)
    elif alone:
        wait_alone(eng, sem, value)
    else:
        eng.wait_ge(sem, value)


def exists(n):
    return not isinstance(n, int) or 0 <= n < B


def neighbour(n, h, ahead):
    h = h + ahead
    return (n + h // H if h // H else n), h % H


def entries(eng, step):
    for n in range(-2, 3):
        step(n, n % 2)
    with eng.Fori(1, B // 2 - 2) as i:
        step(2 * i + 1, 1)
        step(2 * i + 2, 0)
    for n in range(B - 3, B + 1):
        step(n, n % 2)


def spread(ap, shape, at):
    return ap.unsqueeze(at).to_broadcast(shape)


def condition_and_route(nc, ctx, io, keep):
    sems = {}

    def sem(name):
        if name not in sems:
            sems[name] = ctx.enter_context(nc.semaphore(name))
        return sems[name]

    def sb(name, shape, dt=F32):
        return ctx.enter_context(nc.sbuf_tensor(name, shape, dt))

    def bank(name):
        return ctx.enter_context(nc.psum_tensor(name, [P, 512], F32))

    const, vec = keep["const"], keep["vec"]
    ident = const[:, IDENT:IDENT + P]
    below = const[:, BELOW:BELOW + P]
    ones = const[:, ONES:ONES + P]
    slot8 = const[:, SLOT:SLOT + E]
    region_row = const[:, REGION_ROW:REGION_ROW + E]
    gates, out_row = keep["gates"], keep["out_row"]

    w1 = sb("w1", [P, E, C * FF])
    w2 = sb("w2", [P, E, F * D])
    b1 = sb("b1_rows", [P, E, FF])
    b2 = sb("b2_rows", [P, E, D])
    router = sb("router", [P, C, E])
    zeros = sb("zeros", [P, D])

    xin = [sb(f"xin{i}", [P, J, D]) for i in range(2)]
    row_stats = sb("row_stats", [P, J, 6])
    row_mv = sb("row_mv", [P, J, 2])
    row_rstd = sb("row_rstd", [P, J])
    col_stats = sb("col_stats", [P, C, 6])
    col_mv = sb("col_mv", [P, C, 2])
    col_rstd = sb("col_rstd", [P, C])
    col_scale = sb("col_scale", [P, C])
    col_mean_s = sb("col_mean_s", [P, C])
    col_shift = sb("col_shift", [P, C])
    minus_half = sb("minus_half", [P, 2])
    gamma = sb("gamma", [P, C, B])
    beta = sb("beta", [P, C, B])
    columns = sb("columns", [P, 2, C * T])
    hT, h2T = [columns[:, i, :].rearrange("p (c t) -> p c t", c=C) for i in range(2)]
    token_rows = sb("token_rows", [P, 2, J * D])
    h2 = [token_rows[:, i, :].rearrange("p (j d) -> p j d", j=J) for i in range(2)]
    logits = sb("logits", [P, J, E])
    best = sb("best", [P, J, E])
    best_at = sb("best_at", [P, J, E], U32)
    gap = sb("gap", [P, J])
    gap_exp = sb("gap_exp", [P, J])
    gap_sum = sb("gap_sum", [P, J])
    chosen = sb("chosen", [P, K, J])
    onehot = sb("onehot", [P, K * J, E])
    picked = sb("picked", [P, J, E])
    count = sb("count", [P, E])
    rank_base = sb("rank_base", [P, J, E])
    count_mid = sb("count_mid", [P, E])
    rank_sel = sb("rank_sel", [P, K * J, E])
    row_f = sb("row_f", [P, K * J])
    row_i = [sb(f"row_i{i}", [P, K * J], U32) for i in range(2)]
    chosen_all = sb("chosen_all", [P, B, K * J])
    row_all = sb("row_all", [P, B, K * J])
    tiles_n = sb("tiles_n", [P, E])
    tiles_cum = [sb(f"tiles_cum{i}", [P, E]) for i in range(2)]
    delta = sb("delta", [P, E])
    pad_f = sb("pad_f", [P, E])
    pad_i = sb("pad_i", [P, E], U32)
    tile_e = sb("tile_e", [1, TILES])
    tile_ok = sb("tile_ok", [1, TILES])
    tile_row = sb("tile_row", [1, TILES])
    tile_tab = sb("tile_tab", [1, 2, TILES], I32)
    htok = [xin[0][:, i, :] for i in range(2)]
    y = xin[1][:, 0, :]
    htokT = keep["xn"][:, 0, :].rearrange("p (c m) -> p c m", c=C)
    hid = token_rows[:].rearrange("p i n -> p (i n)")
    hidT = columns[:].rearrange("p i n -> p (i n)")
    big = sb("big", [P, B * K * J, E])
    tiles = sb("tiles", [1, TILES, E])

    ps_t, ps_h0, ps_h1, ps_th0, ps_th1, ps_y = [bank(n) for n in ("ps_t", "ps_h0", "ps_h1", "ps_th0", "ps_th1", "ps_y")]
    ps_logit, ps_rank, ps_back = ps_th0, ps_th1, ps_y
    ps_h, ps_th = [ps_h0, ps_h1], [ps_th0, ps_th1]

    x_rows = io["x"].rearrange("(b j p) d -> b p j d", j=J, p=P)
    dispatch, expert_out = io["dispatch"], io["expert_out"]

    consts_in = keep["consts_in"]
    consts_need = 16 * 2
    cond = cond_weights(nc, sb)

    block = ctx.enter_context(nc.Block())

    @block.sync
    def _(sp):
        sp.dma_start(const[:], io["const"]).then_inc(consts_in, 16)
        sp.dma_start(vec[:], io["vec"]).then_inc(consts_in, 16)
        for i in range(2):
            sp.dma_start(xin[i][:], x_rows[i]).then_inc(sem(f"x_in{i}"), 16)
        sp.dma_start(cond["t_int"][:], io["timestep"].partition_broadcast(P)).then_inc(sem("cond_in"), 16)
        sp.dma_start(cond["ids"][:], io["subject"]).then_inc(sem("ids_in"), 16)
        sp.dma_start(cond["hyp_w1"][:], io["hyp_w1"]).then_inc(sem("cond_in"), 16)
        sp.dma_start(cond["hyp_w2"][:], io["hyp_w2"]).then_inc(sem("cond_in"), 16)
        sp.dma_start(cond["sty_w1"][:], io["sty_w1"]).then_inc(sem("cond_in"), 16)
        sp.dma_start(cond["sty_w2"][:], io["sty_w2"]).then_inc(sem("cond_in"), 16)
        sp.dma_start(cond["ada_w"][:], io["ada_w"]).then_inc(sem("cond_in"), 16)
        sp.dma_start(router[:], io["router"]).then_inc(sem("router_in"), 16)
        with sp.Fori(1, B // 2) as i:
            for par in range(2):
                wait_alone(sp, sem("xn_ready"), J * (2 * i + par - 1))
                sp.dma_start(xin[par][:], x_rows[bass.ds(2 * i + par, 1)].rearrange("b p j d -> p (b j) d")
                             ).then_inc(sem(f"x_in{par}"), 16)

        for par in range(2):
            sp.wait_ge(sem(f"row_sent{par}"), 16 * K * J * (B // 2))
        sp.wait_ge(sem("pad_sent"), 16 * E)
        sp.wait_ge(sem("tables_ready"), 1)

        def load(tile):
            row = sp.value_load(tile_tab[0:1, 1, bass.ds(tile.t, 1)], min_val=0, max_val=E * REGION - P)
            sp.dma_start(htok[tile.par], dispatch[bass.ds(row, P), :]).then_inc(sem(f"tile_in{tile.par}"), 16)

        def store(t):
            sp.wait_ge(sem("y_ready"), t + 1)
            sp.dma_start(expert_out[bass.ds(t * P, P), :], y).then_inc(sem("y_sent"), 16)

        def body(tile):
            if not isinstance(tile.t, int) or tile.t + 2 < TILES:
                sp.wait_ge(sem("tile_turned"), tile.t + 1)
                load(tile.ahead(2))
            store(tile.t - 1)

        load(Tile(0, 0))
        load(Tile(0, 1))
        for t in range(2):
            sp.wait_ge(sem("tile_turned"), t + 1)
            load(Tile(0, t + 2))
        store(0)
        tile_loop(sp, body)
        store(TILES - 2)
        store(TILES - 1)
        sp.wait_ge(sem("y_sent"), 16 * TILES)

    @block.gpsimd
    def _(pool):
        pool.memset(minus_half[:], -0.5).then_inc(sem("half_set"), 1)
        pool.memset(zeros[:], 0.0).then_inc(sem("zeros_set"), 1)
        pool.wait_ge(sem("half_set"), 1)
        pool.wait_ge(sem("ids_in"), 16)
        pool.indirect_dma_start(cond["emb"][0:B, :], None, io["subj_emb"],
                                bass.IndirectOffsetOnAxis(ap=cond["ids"][:, 0:1], axis=0),
                                bounds_check=SUBJ - 1, oob_is_err=False).then_inc(sem("emb_in"), 16)

        def row_rsqrt(b):
            pool.wait_ge(sem("row_var_ready"), b + 1)
            if not (isinstance(b, int) and b == 0):
                pool.wait_ge(sem("xn_ready"), J * b)
            pool.tensor_tensor(row_rstd[:], row_mv[:, :, 1], minus_half[:, 0:J], ALU.pow).then_inc(sem("row_rstd_ready"), 1)

        def col_rsqrt(b):
            pool.wait_ge(sem("col_var_ready"), b + 1)
            pool.tensor_tensor(col_rstd[:], col_mv[:, :, 1], minus_half[:, 0:C], ALU.pow).then_inc(sem("col_rstd_ready"), 1)

        def send_rows(b, par):
            wait_alone(pool, sem("row_i_ready"), b + 1)
            wait_alone(pool, sem("h2_ready"), b + 1)
            for k in range(K):
                for j in range(J):
                    q = k * J + j
                    pool.indirect_dma_start(dispatch, bass.IndirectOffsetOnAxis(ap=row_i[par][:, q:q + 1], axis=0),
                                            h2[par][:, j, :], None,
                                            bounds_check=E * REGION - 1, oob_is_err=False).then_inc(sem(f"row_sent{par}"), 16)

        def step(i, par, rows, cols, routed):
            b = 2 * i + par
            if rows:
                row_rsqrt(b)
            if cols:
                col_rsqrt(b - 1)
            if routed:
                send_rows(b - 2, par)

        pipeline(pool, step)
        pool.wait_ge(sem("zeros_set"), 1)
        pool.wait_ge(sem("pad_ready"), 1)
        for e in range(E):
            pool.indirect_dma_start(dispatch, bass.IndirectOffsetOnAxis(ap=pad_i[:, e:e + 1], axis=0),
                                    zeros[:], None,
                                    bounds_check=E * REGION - 1, oob_is_err=False).then_inc(sem("pad_sent"), 16)

    @block.scalar
    def _(act):
        act.dma_start(b1[:], io["b1"].partition_broadcast(P)).then_inc(sem("w_in"), 16)
        act.dma_start(b2[:], io["b2"].partition_broadcast(P)).then_inc(sem("w_in"), 16)
        cond_scalar(nc, act, cond, vec, sem)

        def load_experts(b):
            for dst, src in ((w1, io["w1"]), (w2, io["w2"])):
                dst, src = [ap.rearrange("p e (i n) -> p (e i) n", i=2)[:, bass.ds(b, 1), :] for ap in (dst[:], src)]
                act.dma_start(dst, src).then_inc(sem("w_in"), 16)

        def step(i, par, rows, cols, routed):
            b = 2 * i + par
            if rows:
                load_experts(b)
            if routed:
                act.wait_ge(sem("gap_ready"), b - 1)
                act.activation(gap_exp[:], gap[:], ACT.Exp).then_inc(sem("gap_exp_ready"), 1)
            if rows:
                act.wait_ge(sem("xnT_done"), b + 1)
                if not (isinstance(b, int) and b == 0):
                    act.wait_ge(sem("h2T_ready"), b)
                for c in range(C):
                    act.activation(hT[:, c, :], ps_t[:, c * T:(c + 1) * T], ACT.Identity, bias=vec[:, LN_B + c:LN_B + c + 1],
                                   scale=vec[:, LN_G + c:LN_G + c + 1]).then_inc(sem("hT_ready"), 1)
            if cols:
                p = 1 - par
                own = i if par else i - 1
                act.wait_ge(sem("back_done"), b)
                if not (isinstance(own, int) and own == 0):
                    act.wait_ge(sem(f"row_sent{p}"), 16 * K * J * own)
                act.activation(h2[p], ps_back[:, :].rearrange("p (j d) -> p j d", j=J), ACT.Copy).then_inc(sem("h2_ready"), 1)

        pipeline(act, step)

        def take_in(t):
            act.wait_ge(sem("tile_turned"), t + 1)
            if not (isinstance(t, int) and t == 0):
                act.wait_ge(sem("up_done"), 2 * t)
            act.activation(htokT, ps_t[:, 0:C * P].rearrange("p (c m) -> p c m", c=C), ACT.Copy).then_inc(sem("htokT_ready"), 1)

        def relu(t):
            act.wait_ge(sem("hid_turned"), t + 1)
            if not (isinstance(t, int) and t == 0):
                act.wait_ge(sem("down_done"), t)
            for i in range(2):
                act.activation(hidT[:, i * 512:(i + 1) * 512], ps_th[i][:, :], ACT.Relu).then_inc(sem("hidT_ready"), 1)

        take_in(0)
        take_in(1)
        relu(0)
        take_in(2)

        def body(tile):
            relu(tile.t - 1)
            take_in(tile.t + 1)

        tile_loop(act, body)
        relu(TILES - 2)
        relu(TILES - 1)

    @block.tensor
    def _(pe):
        pe.wait_ge(consts_in, consts_need)
        cond_tensor(nc, pe, cond, ident, ps_h0, ps_h1, sem)
        pe.wait_ge(sem("router_in"), 16)

        def step(i, par, rows, cols, routed):
            b = 2 * i + par
            if routed:
                pe.wait_ge(sem("picked_ready"), b - 1)
                pe.matmul(ps_rank[:, 0:J * E], below, picked[:].rearrange("p j e -> p (j e)"), start=True, stop=True)
                pe.matmul(ps_rank[:, J * E:2 * J * E], ones, picked[:].rearrange("p j e -> p (j e)"),
                          start=True, stop=True).then_inc(sem("rank_done"), 1)
            if rows:
                pe.wait_ge(sem("xn_ready"), J * (b + 1))
                if not (isinstance(b, int) and b == 0):
                    pe.wait_ge(sem("hT_ready"), C * b)
                for c in range(C):
                    for j in range(J):
                        last = pe.transpose(ps_t[:, c * T + j * P:c * T + (j + 1) * P], xin_n[:, j, c * P:(c + 1) * P], ident)
                last.then_inc(sem("xnT_done"), 1)
            if cols:
                pe.wait_ge(sem("h2T_ready"), b)
                if not (isinstance(b, int) and b == 1):
                    pe.wait_ge(sem("logits_taken"), b - 1)
                for j in range(J):
                    for c in range(C):
                        last = pe.matmul(ps_logit[:, j * E:(j + 1) * E], h2T[:, c, j * P:(j + 1) * P], router[:, c, :],
                                         start=(c == 0), stop=(c == C - 1))
                last.then_inc(sem("logits_done"), 1)
                if not (isinstance(b, int) and b == 1):
                    pe.wait_ge(sem("h2_ready"), b - 1)
                for j in range(J):
                    for c in range(C):
                        last = pe.transpose(ps_back[:, j * D + c * P:j * D + (c + 1) * P], h2T[:, c, j * P:(j + 1) * P], ident)
                last.then_inc(sem("back_done"), 1)

        xin_n = keep["xn"]
        pipeline(pe, step)

        def expert_of(t):
            return pe.value_load(tile_tab[0:1, 0, bass.ds(t, 1)], min_val=0, max_val=E - 1)

        def turn_in(tile):
            t = tile.t
            pe.wait_ge(sem(f"tile_in{tile.par}"), 16 * (tile.before + 1))
            if isinstance(t, int) and t == 0:
                pe.wait_ge(sem("h2_ready"), B)
                pe.wait_ge(sem("hT_ready"), C * B)
            else:
                pe.wait_ge(sem("htokT_ready"), t)
            for c in range(C):
                last = pe.transpose(ps_t[:, c * P:(c + 1) * P], htok[tile.par][:, c * P:(c + 1) * P], ident)
            last.then_inc(sem("tile_turned"), 1)

        def up(t, e):
            pe.wait_ge(sem("htokT_ready"), t + 1)
            if not (isinstance(t, int) and t == 0):
                pe.wait_ge(sem("hid_ready"), 2 * t)
            for i in range(2):
                for c in range(C):
                    last = pe.matmul(ps_h[i][:, :], htokT[:, c, :],
                                     w1[:, bass.ds(e, 1), c * FF + i * 512:c * FF + (i + 1) * 512].rearrange("p e n -> p (e n)"),
                                     start=(c == 0), stop=(c == C - 1))
                last.then_inc(sem("up_done"), 1)

        def turn_hidden(t):
            pe.wait_ge(sem("hid_ready"), 2 * (t + 1))
            if not (isinstance(t, int) and t == 0):
                pe.wait_ge(sem("hidT_ready"), 2 * t)
            for f in range(F):
                last = pe.transpose(ps_th[f // 4][:, (f % 4) * P:(f % 4 + 1) * P], hid[:, f * P:(f + 1) * P], ident)
            last.then_inc(sem("hid_turned"), 1)

        def down(t, e):
            pe.wait_ge(sem("hidT_ready"), 2 * (t + 1))
            if not (isinstance(t, int) and t == 0):
                pe.wait_ge(sem("y_ready"), t)
            for f in range(F):
                last = pe.matmul(ps_y[:, 0:D], hidT[:, f * P:(f + 1) * P],
                                 w2[:, bass.ds(e, 1), f * D:(f + 1) * D].rearrange("p e n -> p (e n)"),
                                 start=(f == 0), stop=(f == F - 1))
            last.then_inc(sem("down_done"), 1)

        pe.wait_ge(sem("w_in"), 16 * (2 * B + 2))
        pe.wait_ge(sem("tables_ready"), 1)
        e0 = expert_of(0)
        turn_in(Tile(0, 0))
        up(0, e0)
        turn_in(Tile(0, 1))
        turn_hidden(0)
        e1 = expert_of(1)
        up(1, e1)
        turn_in(Tile(0, 2))
        down(0, e0)

        def body(tile):
            t = tile.t
            before, now = expert_of(t - 1), expert_of(t)
            turn_hidden(t - 1)
            up(t, now)
            turn_in(tile.ahead(1))
            down(t - 1, before)

        tile_loop(pe, body)
        before, now = expert_of(TILES - 2), expert_of(TILES - 1)
        turn_hidden(TILES - 2)
        up(TILES - 1, now)
        down(TILES - 2, before)
        turn_hidden(TILES - 1)
        down(TILES - 1, now)

    @block.vector
    def _(dve):
        xn = keep["xn"]
        dve.wait_ge(consts_in, consts_need)
        cond_vector(nc, dve, cond, vec, ps_h0, ps_h1, gamma, beta, keep, sem)
        dve.tensor_copy(count[:], region_row).then_inc(sem("count_ready"), 1)
        dve.wait_ge(sem("count_ready"), 1)

        def row_moments(b, i, par):
            dve.wait_ge(sem(f"x_in{par}"), 16 * (i + 1))
            for j in range(J):
                last = dve.bn_stats(row_stats[:, j, :], xin[par][:, j, :])
            last.then_inc(sem("row_stats_done"), 1)
            wait_free(dve, sem("row_rstd_ready"), b, alone=True)
            wait_alone(dve, sem("row_stats_done"), b + 1)
            for j in range(J):
                last = dve.bn_aggr(row_mv[:, j, :], row_stats[:, j, :])
            last.then_inc(sem("row_mv_done"), 1)
            dve.wait_ge(sem("row_mv_done"), b + 1)
            dve.tensor_scalar(row_mv[:, :, 1], row_mv[:, :, 1], 1e-5, None, ALU.add).then_inc(sem("row_var_ready"), 1)

        def normalise_rows(b, par):
            dve.wait_ge(sem("row_rstd_ready"), b + 1)
            if not (isinstance(b, int) and b == 0):
                dve.wait_ge(sem("xnT_done"), b)
            for j in range(J):
                dve.tensor_scalar(xn[:, j, :], xin[par][:, j, :], row_mv[:, j, 0:1], row_rstd[:, j:j + 1],
                                  ALU.subtract, ALU.mult).then_inc(sem("xn_ready"), 1)

        def column_moments(b):
            dve.wait_ge(sem("hT_ready"), C * (b + 1))
            for c in range(C):
                last = dve.bn_stats(col_stats[:, c, :], hT[:, c, :])
            last.then_inc(sem("col_stats_done"), 1)
            wait_alone(dve, sem("col_stats_done"), b + 1)
            for c in range(C):
                last = dve.bn_aggr(col_mv[:, c, :], col_stats[:, c, :])
            last.then_inc(sem("col_mv_done"), 1)
            dve.wait_ge(sem("col_mv_done"), b + 1)
            dve.tensor_scalar(col_mv[:, :, 1], col_mv[:, :, 1], 1e-8, None, ALU.add).then_inc(sem("col_var_ready"), 1)

        def modulate_columns(b):
            dve.wait_ge(sem("col_rstd_ready"), b + 1)
            s = Steps(dve, sem("col_step"), 3 * b)
            s.then(dve.tensor_tensor(col_scale[:], col_rstd[:], gamma[:, :, bass.ds(b, 1)].rearrange("p c b -> p (c b)"), ALU.mult))
            s.then(dve.tensor_tensor(col_mean_s[:], col_mv[:, :, 0], col_scale[:], ALU.mult))
            s.then(dve.tensor_tensor(col_shift[:], beta[:, :, bass.ds(b, 1)].rearrange("p c b -> p (c b)"), col_mean_s[:], ALU.subtract))
            if not (isinstance(b, int) and b == 0):
                dve.wait_ge(sem("back_done"), b)
            for c in range(C):
                last = dve.tensor_scalar(h2T[:, c, :], hT[:, c, :], col_scale[:, c:c + 1], col_shift[:, c:c + 1], ALU.mult, ALU.add)
            last.then_inc(sem("h2T_ready"), 1)

        ROUTE_STEPS = 16

        def route(b, own, par):
            s = Steps(dve, sem("route_step"), ROUTE_STEPS * b)
            dve.wait_ge(sem("logits_done"), b + 1)
            dve.tensor_copy(logits[:], ps_logit[:, 0:J * E].rearrange("p (j e) -> p j e", j=J)).then_inc(sem("logits_taken"), 1)
            wait_alone(dve, sem("logits_taken"), b + 1)
            for j in range(J):
                last = dve.max(best[:, j, :], logits[:, j, :])
            s.then_alone(last)
            for j in range(J):
                last = dve.max_index(best_at[:, j, :], best[:, j, :], logits[:, j, :])
            s.did(last)
            dve.tensor_tensor(gap[:], best[:, :, 1], best[:, :, 0], ALU.subtract).then_inc(sem("gap_ready"), 1)
            dve.wait_ge(sem("route_step"), s.at)
            s.then(dve.tensor_copy(chosen[:], best_at[:, :, 0:K].rearrange("p j k -> p k j")))
            choice = chosen[:].rearrange("p k j -> p (k j)")
            s.then(dve.tensor_tensor(onehot[:], spread(choice, [P, K * J, E], 2), spread(slot8, [P, K * J, E], 1), ALU.is_equal))
            dve.tensor_tensor(picked[:], onehot[:, 0:J, :], onehot[:, J:2 * J, :], ALU.add).then_inc(sem("picked_ready"), 1)
            s.did(dve.tensor_copy(chosen_all[:, bass.ds(b, 1), :].rearrange("p b q -> p (b q)"), choice))
            dve.wait_ge(sem("gap_exp_ready"), b + 1)
            s.then(dve.tensor_scalar(gap_sum[:], gap_exp[:], 1.0, None, ALU.add))
            first = gates[:, bass.ds(b, 1), 0, :].rearrange("p b j -> p (b j)")
            second = gates[:, bass.ds(b, 1), 1, :].rearrange("p b j -> p (b j)")
            s.then(dve.reciprocal(gap_sum[:], gap_sum[:]))
            s.did(dve.tensor_tensor(second, gap_exp[:], gap_sum[:], ALU.mult))
            s.did(dve.tensor_copy(first, gap_sum[:]))
            dve.wait_ge(sem("rank_done"), b + 1)
            n = J * E
            s.did(dve.tensor_tensor(rank_base[:, 0, :], ps_rank[:, 0:E], count[:], ALU.add))
            s.then(dve.tensor_tensor(count_mid[:], ps_rank[:, n:n + E], count[:], ALU.add))
            s.did(dve.tensor_tensor(rank_base[:, 1, :], ps_rank[:, E:2 * E], count_mid[:], ALU.add))
            s.then(dve.tensor_tensor(count[:], ps_rank[:, n + E:n + 2 * E], count_mid[:], ALU.add))
            s.then(dve.tensor_tensor(rank_sel[:].rearrange("p (k j) e -> p k j e", k=K), onehot[:].rearrange("p (k j) e -> p k j e", k=K),
                                     spread(rank_base[:], [P, K, J, E], 1), ALU.mult))
            s.then(dve.tensor_reduce(row_f[:], rank_sel[:], X, ALU.add))
            s.did(dve.tensor_copy(row_all[:, bass.ds(b, 1), :].rearrange("p b q -> p (b q)"), row_f[:]))
            if not (isinstance(own, int) and own == 0):
                dve.wait_ge(sem(f"row_sent{par}"), 16 * K * J * own)
            dve.tensor_copy(row_i[par][:], row_f[:]).then_inc(sem("row_i_ready"), 1)

        def step(i, par, rows, cols, routed):
            b = 2 * i + par
            if rows:
                row_moments(b, i, par)
            if cols:
                column_moments(b - 1)
            if routed:
                route(b - 2, i - 1, par)
            if rows:
                normalise_rows(b, par)
            if cols:
                modulate_columns(b - 1)

        pipeline(dve, step)

        s = Steps(dve, sem("table_step"))
        s.did(dve.tensor_scalar(pad_f[:], count[:], vec[:, PART:PART + 1], None, ALU.add))
        s.then(dve.tensor_tensor(tiles_n[:], count[:], region_row, ALU.subtract))
        dve.tensor_copy(pad_i[:], pad_f[:]).then_inc(sem("pad_ready"), 1)
        s.then(dve.tensor_scalar(tiles_n[:], tiles_n[:], float(P - 1), 1.0 / P, ALU.add, ALU.mult))
        s.then(dve.tensor_scalar(tiles_n[:], tiles_n[:], -(P - 1) / (2.0 * P), MAGIC, ALU.add, ALU.add))
        s.then(dve.tensor_scalar(tiles_n[:], tiles_n[:], -MAGIC, None, ALU.add))
        s.then(dve.tensor_copy(tiles_cum[0][:], tiles_n[:]))
        now = 0
        for shift in (1, 2, 4):
            s.did(dve.tensor_copy(tiles_cum[1 - now][:, 0:shift], tiles_cum[now][:, 0:shift]))
            s.then(dve.tensor_tensor(tiles_cum[1 - now][:, shift:E], tiles_cum[now][:, shift:E], tiles_cum[now][:, 0:E - shift], ALU.add))
            now = 1 - now
        cum = tiles_cum[now]
        s.then(dve.tensor_tensor(delta[:], cum[:], tiles_n[:], ALU.subtract))
        s.then(dve.tensor_scalar(delta[:], delta[:], float(P), None, ALU.mult))
        s.then(dve.tensor_tensor(delta[:], delta[:], region_row, ALU.subtract))
        tile_no = const[0:1, TILE_NO:TILE_NO + TILES]
        s.then(dve.tensor_tensor(tiles[:], spread(tile_no, [1, TILES, E], 2), spread(cum[0:1, :], [1, TILES, E], 1), ALU.is_ge))
        s.then(dve.tensor_reduce(tile_e[:], tiles[:], X, ALU.add))
        s.then(dve.tensor_scalar(tile_e[:], tile_e[:], float(E - 1), None, ALU.min))
        s.then(dve.tensor_tensor(tiles[:], spread(tile_e[:], [1, TILES, E], 2), spread(slot8[0:1, :], [1, TILES, E], 1), ALU.is_equal))
        s.then(dve.tensor_tensor(tiles[:], tiles[:], spread(delta[0:1, :], [1, TILES, E], 1), ALU.mult))
        s.did(dve.tensor_reduce(tile_row[:], tiles[:], X, ALU.add))
        s.then(dve.tensor_scalar(tile_ok[:], tile_no, cum[0:1, E - 1:E], None, ALU.is_lt))
        s.then(dve.scalar_tensor_tensor(tile_row[:], tile_no, float(P), tile_row[:], ALU.mult, ALU.subtract))
        s.then(dve.tensor_tensor(tile_row[:], tile_row[:], tile_ok[:], ALU.mult))
        s.did(dve.tensor_copy(tile_tab[:, 0, :], tile_e[:]))
        dve.tensor_copy(tile_tab[:, 1, :], tile_row[:]).then_inc(sem("tables_ready"), 1)
        every = chosen_all[:].rearrange("p b q -> p (b q)")
        s.then(dve.tensor_tensor(big[:], spread(every, [P, B * K * J, E], 2), spread(slot8, [P, B * K * J, E], 1), ALU.is_equal))
        s.then(dve.tensor_tensor(big[:], big[:], spread(delta[:], [P, B * K * J, E], 1), ALU.mult))
        s.then(dve.tensor_reduce(every, big[:], X, ALU.add))
        s.then(dve.tensor_tensor(every, every, row_all[:].rearrange("p b q -> p (b q)"), ALU.add))
        s.did(dve.tensor_copy(out_row[:], chosen_all[:]))

        dve.wait_ge(sem("w_in"), 16 * (2 * B + 2))
        dve.wait_ge(sem("tables_ready"), 1)

        def expert_of(t):
            return dve.value_load(tile_tab[0:1, 0, bass.ds(t, 1)], min_val=0, max_val=E - 1)

        def take_hidden(t, e):
            for i in range(2):
                dve.wait_ge(sem("up_done"), 2 * t + i + 1)
                if i == 0 and not (isinstance(t, int) and t == 0):
                    dve.wait_ge(sem("hid_turned"), t)
                dve.tensor_tensor(hid[:, i * 512:(i + 1) * 512], ps_h[i][:, :],
                                  b1[:, bass.ds(e, 1), i * 512:(i + 1) * 512].rearrange("p e n -> p (e n)"),
                                  ALU.add).then_inc(sem("hid_ready"), 1)

        def take_out(t, e):
            dve.wait_ge(sem("down_done"), t + 1)
            if not (isinstance(t, int) and t == 0):
                dve.wait_ge(sem("y_sent"), 16 * t)
            dve.tensor_tensor(y, ps_y[:, 0:D], b2[:, bass.ds(e, 1), :].rearrange("p e n -> p (e n)"), ALU.add).then_inc(sem("y_ready"), 1)

        e0, e1 = expert_of(0), expert_of(1)
        take_hidden(0, e0)
        take_hidden(1, e1)
        take_out(0, e0)

        def body(tile):
            t = tile.t
            before, now = expert_of(t - 1), expert_of(t)
            take_hidden(t, now)
            take_out(t - 1, before)

        tile_loop(dve, body)
        body(Tile(0, TILES - 1))
        take_out(TILES - 1, expert_of(TILES - 1))


UNROLL = 4


class Tile:

    def __init__(self, round_, offset):
        self.round, self.offset = round_, offset
        self.t = UNROLL * round_ + offset
        self.par = offset % 2
        self.before = UNROLL // 2 * round_ + offset // 2

    def ahead(self, n):
        return Tile(self.round, self.offset + n)


def tile_loop(eng, body):
    rounds = (TILES - 3) // UNROLL - 1
    with eng.Fori(0, rounds) as i:
        for u in range(2, 2 + UNROLL):
            body(Tile(i, u))
    for t in range(2 + rounds * UNROLL, TILES - 1):
        body(Tile(0, t))


def pipeline(eng, step):
    step(0, 0, True, False, False)
    step(0, 1, True, True, False)
    step(1, 0, True, True, True)
    step(1, 1, True, True, True)
    with eng.Fori(2, B // 2) as i:
        step(i, 0, True, True, True)
        step(i, 1, True, True, True)
    step(B // 2, 0, False, True, True)
    step(B // 2, 1, False, False, True)


def cond_weights(nc, sb):
    return {
        "ids": sb("ids", [B, 1], U32), "emb": sb("emb", [B, SE]), "embT": sb("embT", [SE, B]),
        "hyp_w1": sb("hyp_w1", [SE, SH]), "hyp_w2": sb("hyp_w2", [SH, SH]),
        "sty_w1": sb("sty_w1", [SH, SH // 2]), "sty_w2": sb("sty_w2", [SH // 2, 2 * D]),
        "ada_w": sb("ada_w", [P, C, 2 * D]),
        "a1": sb("a1", [SH, B]), "a2": sb("a2", [SH, B]), "a3": sb("a3", [SH // 2, B]),
        "pre": sb("pre", [P, C, B]), "neg": sb("neg", [P, C, B]), "low": sb("low", [P, C, B]),
        "exp": sb("exp", [P, C, B]), "log": sb("log", [P, C, B]),
        "t_int": sb("t_int", [P, B], I32), "t": sb("t", [P, B]), "q": sb("q", [P, B]), "qh": sb("qh", [P, B]),
        "ql": sb("ql", [P, B]), "r": sb("r", [P, B]), "angle": sb("angle", [P, 2, B]), "turns": sb("turns", [P, 2, B]),
        "wave": sb("wave", [P, 2, B]), "half": sb("half", [P, 2, B]),
    }


def cond_tensor(nc, pe, w, ident, ps_a, ps_b, sem):
    pe.wait_ge(sem("emb_in"), 16)
    pe.wait_ge(sem("cond_in"), 16 * 6)
    pe.transpose(ps_a[0:SE, 0:B], w["emb"][:, :], ident[0:B, 0:B]).then_inc(sem("cond_product"), 1)
    pe.wait_ge(sem("cond_layer"), 1)
    pe.matmul(ps_b[0:SH, 0:B], w["hyp_w1"][:, :], w["embT"][:, :], start=True, stop=True).then_inc(sem("cond_product"), 1)
    pe.wait_ge(sem("cond_layer"), 2)
    pe.matmul(ps_a[0:SH, 0:B], w["hyp_w2"][:, :], w["a1"][:, :], start=True, stop=True).then_inc(sem("cond_product"), 1)
    pe.wait_ge(sem("cond_layer"), 3)
    pe.matmul(ps_b[0:SH // 2, 0:B], w["sty_w1"][:, :], w["a2"][:, :], start=True, stop=True).then_inc(sem("cond_product"), 1)
    pe.wait_ge(sem("cond_layer"), 4)
    for m in range(2 * C):
        last = pe.matmul(ps_a[:, m * B:(m + 1) * B], w["sty_w2"][:, m * P:(m + 1) * P], w["a3"][:, :], start=True, stop=True)
    last.then_inc(sem("cond_product"), 1)
    pe.wait_ge(sem("wave_ready"), 1)
    for m in range(2 * C):
        for c in range(C):
            last = pe.matmul(ps_b[:, m * B:(m + 1) * B], w["ada_w"][:, c, m * P:(m + 1) * P], w["wave"][:, c, :],
                             start=(c == 0), stop=(c == C - 1))
    last.then_inc(sem("cond_product"), 1)


def cond_scalar(nc, act, w, vec, sem):
    act.wait_ge(sem("angle_ready"), 1)
    act.activation(w["turns"][:], w["angle"][:], ACT.Sin).then_inc(sem("sine_ready"), 1)
    act.wait_ge(sem("low_ready"), 1)
    act.activation(w["exp"][:], w["low"][:], ACT.Exp).then_inc(sem("soft_exp_ready"), 1)
    act.wait_ge(sem("soft_exp_ready"), 1)
    act.activation(w["log"][:], w["exp"][:], ACT.Ln, bias=1.0).then_inc(sem("soft_log_ready"), 1)
    act.wait_ge(sem("sine_ready"), 1)
    act.activation(w["half"][:], w["turns"][:], ACT.Tanh, scale=0.5).then_inc(sem("tanh_ready"), 1)


def cond_vector(nc, dve, w, vec, ps_a, ps_b, gamma, beta, keep, sem):
    s = Steps(dve, sem("cond_step"))
    dve.wait_ge(sem("cond_in"), 16 * 6)
    s.then(dve.tensor_copy(w["t"][:], w["t_int"][:]))
    s.then(dve.tensor_scalar(w["q"][:], w["t"][:], 0.01, None, ALU.mult))
    s.then(dve.tensor_scalar(w["qh"][:], w["q"][:], 4097.0, None, ALU.mult))
    s.then(dve.tensor_tensor(w["r"][:], w["qh"][:], w["q"][:], ALU.subtract))
    s.then(dve.tensor_tensor(w["qh"][:], w["qh"][:], w["r"][:], ALU.subtract))
    s.then(dve.tensor_tensor(w["ql"][:], w["q"][:], w["qh"][:], ALU.subtract))
    s.then(dve.scalar_tensor_tensor(w["r"][:], w["qh"][:], -100.0, w["t"][:], ALU.mult, ALU.add))
    s.then(dve.scalar_tensor_tensor(w["r"][:], w["ql"][:], -100.0, w["r"][:], ALU.mult, ALU.add))
    s.then(dve.scalar_tensor_tensor(w["q"][:], w["r"][:], 0.01, w["q"][:], ALU.mult, ALU.add))
    s.then(dve.tensor_scalar(w["q"][:], w["q"][:], 4000.0, None, ALU.mult))
    for i in range(2):
        last = dve.tensor_scalar(w["angle"][:, i, :], w["q"][:], vec[:, FREQ:FREQ + 1], None, ALU.mult)
    s.then(last)
    for i in range(2):
        last = dve.tensor_scalar(w["turns"][:, i, :], w["angle"][:, i, :], 1.0 / (2 * np.pi), 0.25 * i, ALU.mult, ALU.add)
    s.then(last)
    s.then(dve.tensor_scalar(w["turns"][:], w["turns"][:], 1.5 * MAGIC, -1.5 * MAGIC, ALU.add, ALU.add))
    two_pi = [6.28125, 0.0019350051879882812, 3.0199159819e-07]
    for part in two_pi:
        s.then(dve.scalar_tensor_tensor(w["angle"][:], w["turns"][:], -part, w["angle"][:], ALU.mult, ALU.add))
    s.then(dve.tensor_scalar(w["angle"][:, 1, :], w["angle"][:, 1, :], float(np.pi / 2), None, ALU.add))
    dve.tensor_scalar(w["angle"][:], w["angle"][:], 3.1415925, -3.1415925, ALU.min, ALU.max).then_inc(sem("angle_ready"), 1)
    dve.wait_ge(sem("cond_product"), 1)
    dve.tensor_copy(w["embT"][:], ps_a[0:SE, 0:B]).then_inc(sem("cond_layer"), 1)
    dve.wait_ge(sem("cond_product"), 2)
    dve.tensor_scalar(w["a1"][:], ps_b[0:SH, 0:B], vec[:, HYP_B1:HYP_B1 + 1], 0.0, ALU.add, ALU.max).then_inc(sem("cond_layer"), 1)
    dve.wait_ge(sem("cond_product"), 3)
    dve.tensor_scalar(w["a2"][:], ps_a[0:SH, 0:B], vec[:, HYP_B2:HYP_B2 + 1], None, ALU.add).then_inc(sem("cond_layer"), 1)
    dve.wait_ge(sem("cond_product"), 4)
    dve.tensor_scalar(w["a3"][:], ps_b[0:SH // 2, 0:B], vec[0:SH // 2, STY_B1:STY_B1 + 1], 0.0, ALU.add, ALU.max).then_inc(sem("cond_layer"), 1)
    dve.wait_ge(sem("cond_product"), 5)
    for c in range(C):
        dve.tensor_scalar(w["pre"][:, c, :], ps_a[:, c * B:(c + 1) * B], vec[:, STY_B2 + c:STY_B2 + c + 1], None, ALU.add)
        last = dve.tensor_scalar(beta[:, c, :], ps_a[:, (C + c) * B:(C + c + 1) * B], vec[:, STY_B2 + C + c:STY_B2 + C + c + 1], None, ALU.add)
    s.then(last)
    s.then(dve.tensor_scalar(w["neg"][:], w["pre"][:], -1.0, None, ALU.mult))
    dve.tensor_tensor(w["low"][:], w["pre"][:], w["neg"][:], ALU.min).then_inc(sem("low_ready"), 1)
    dve.wait_ge(sem("soft_log_ready"), 1)
    s.then(dve.scalar_tensor_tensor(gamma[:], w["pre"][:], 0.0, w["log"][:], ALU.max, ALU.add))
    s.then(dve.tensor_scalar(gamma[:], gamma[:], 1e-8, None, ALU.add))
    dve.wait_ge(sem("tanh_ready"), 1)
    s.then(dve.tensor_scalar(w["half"][:], w["half"][:], 1.0, 0.5, ALU.add, ALU.mult))
    dve.tensor_tensor(w["wave"][:], w["half"][:], w["turns"][:], ALU.mult).then_inc(sem("wave_ready"), 1)
    dve.wait_ge(sem("cond_product"), 6)
    for c in range(C):
        dve.tensor_scalar(keep["scale"][:, c, :], ps_b[:, c * B:(c + 1) * B], vec[:, ADA_B + c:ADA_B + c + 1], 1.0, ALU.add, ALU.add)
        last = dve.tensor_scalar(keep["shift"][:, c, :], ps_b[:, (C + c) * B:(C + c + 1) * B],
                                 vec[:, ADA_B + C + c:ADA_B + C + c + 1], None, ALU.add)
    s.then(last)


CHUNK = 4
PIECES = H // CHUNK
def by_scalar(h):
    return h % 4 != 3


def transformer(nc, ctx, io, keep):
    sems = {}

    def sem(name):
        if name not in sems:
            sems[name] = ctx.enter_context(nc.semaphore(name))
        return sems[name]

    def sb(name, shape, dt=F32):
        return ctx.enter_context(nc.sbuf_tensor(name, shape, dt))

    def bank(name):
        return ctx.enter_context(nc.psum_tensor(name, [P, 512], F32))

    const, vec, gates, out_row = keep["const"], keep["vec"], keep["gates"], keep["out_row"]
    scale, shift, xn = keep["scale"], keep["shift"], keep["xn"]
    ident = const[:, IDENT:IDENT + P]
    x_rows = io["x"].rearrange("(b j p) d -> b p j d", j=J, p=P)
    out_rows = io["out"].rearrange("(b j p) d -> b p j d", j=J, p=P)
    bias_rows = io["bias"].rearrange("b h (j p) k -> b p h j k", p=P)
    mask_rows = io["mask"].rearrange("b (j p) k -> b p j k", p=P)

    wq, wk, wv, wo = [sb(n, [P, C, D]) for n in ("wq", "wk", "wv", "wo")]
    w1, w2 = sb("ff1", [P, C, FF]), sb("ff2", [P, F, D])
    bv, bo, b2 = [sb(n, [P, D]) for n in ("bv", "bo", "b2")]
    q_b = sb("q_b", [P, C])
    tanh_b = sb("tanh_b", [P, F])
    minus_half = sb("minus_half2", [P, J])
    row_now = sb("row_now", [P, K * J], U32)
    gate_now = sb("gate_now", [P, K * J])
    mod_now = sb("mod_now", [P, 2, C])
    x = sb("x", [P, J, D])
    picked_rows = sb("picked_rows", [P, K * J, D])
    src = sb("src", [P, J, D])
    stats, mv, rstd = sb("stats", [P, J, 6]), sb("mv", [P, J, 2]), sb("rstd", [P, J])
    xmT = [sb(f"xmT{i}", [P, C, T]) for i in range(2)]
    part = {n: sb(n, [P, C, T], F32R) for n in ("q_hi", "q_lo", "k_hi", "k_lo")}
    q_stack = [sb(f"q_stack{i}", [P, H // 2, T]) for i in range(2)]
    k_stack = [sb(f"k_stack{i}", [P, H // 2, T]) for i in range(2)]
    V_WIDE = (P // HD) * (P + HD)
    v_pad = [sb(f"v_pad{i}", [P, J, C, V_WIDE]) for i in range(2)]
    mask = sb("mask", [P, J, T // 4], U32)
    mask_f = sb("mask_f", [P, J, T])
    bias = sb("bias", [P, PIECES, CHUNK, J * T])
    neg = [sb(f"neg{i}", [P, J, T]) for i in range(2)]
    neg_max = [sb(f"neg_max{i}", [P, H, J]) for i in range(2)]
    total = [sb(f"total{i}", [P, H, J]) for i in range(2)]
    prob = [sb(f"prob{i}", [P, J, T]) for i in range(4)]
    probT = [sb(f"probT{i}", [P, J, T]) for i in range(4)]
    undefined = sb("undefined", [P, H, J])
    inv = sb("inv", [P, J, H])
    invT = sb("invT", [H, T])
    ctx_raw = sb("ctx_raw", [P, C, T])
    ctxT = sb("ctxT", [P, C, T])
    x3 = sb("x3", [P, J, D])
    x3b = sb("x3b", [P, J, D])
    stats2, mv2, rstd2 = sb("stats2", [P, J, 6]), sb("mv2", [P, J, 2]), sb("rstd2", [P, J])
    h_rows = sb("h_rows", [P, J, D])
    hT = sb("hT", [P, C, T])
    tanh_f = sb("tanh_f", [P, 4, T])
    up_f = sb("up_f", [P, 4, T])
    act_f = sb("act_f", [P, F, T])
    result = sb("result", [P, J, D])

    ps_s = [bank(f"ps_s{i}") for i in range(2)]
    ps_p = [bank(f"ps_p{i}") for i in range(2)]
    ps_ctx = [bank(f"ps_ctx{i}") for i in range(2)]
    ps_g = [bank(f"ps_g{i}") for i in range(2)]

    def halves(ap):
        return ap.rearrange("p (i n) -> p i n", i=2)

    block = ctx.enter_context(nc.Block())

    @block.sync
    def _(sp):
        def load_x(n):
            wait_free(sp, sem("src_read"), n, alone=True)
            sp.dma_start(x[:], x_rows[bass.ds(n, 1)].rearrange("b p j d -> p (b j) d")).then_inc(sem("x2_in"), 16)

        def load_mask(n):
            wait_free(sp, sem("mask_taken"), n, alone=True)
            sp.dma_start(mask[:], mask_rows[bass.ds(n, 1)].rearrange("b p j k -> p (b j) k")).then_inc(sem("mask_in"), 16)

        def load_bias(n, c):
            wait_free(sp, sem("neg_ready"), J * (H * (n - 1) + CHUNK * (c + 1)), alone=True)
            sp.dma_start(bias[:, c, :, :].rearrange("p h (j k) -> p h j k", j=J),
                         bias_rows[bass.ds(n, 1), :, c * CHUNK:(c + 1) * CHUNK].rearrange("b p h j k -> p (b h) j k")
                         ).then_inc(sem(f"bias_in{c}"), 16)

        def stack(n, par):
            wait_free(sp, sem("stack_in"), 16 * 16 * n, alone=True)
            for which in ("q", "k"):
                sp.wait_ge(sem(f"{which}_split"), 2 * C * (n + 1))
                for piece in ("hi", "lo"):
                    name = f"{which}_{piece}"
                    sp.dma_start(io[name].rearrange("(m p) t -> p m t", p=P), part[name][:].bitcast(F32)).then_inc(sem("split_sent"), 16)
            sp.wait_ge(sem("split_sent"), 64 * (n + 1))
            if n_int_or(n) >= 2:
                sp.wait_ge(sem("scores_done"), H * (n - 1))
            for which, dst, order in (("q", q_stack[par], ("hi", "lo", "hi", "lo")), ("k", k_stack[par], ("hi", "hi", "lo", "lo"))):
                for term, piece in enumerate(order):
                    rows = io[f"{which}_{piece}"].rearrange("(s i d) t -> i d s t", i=2, d=HD)
                    for i in range(2):
                        at = i * 64 + term * HD
                        sp.dma_start(dst[at:at + HD, :, :], rows[i]).then_inc(sem("stack_in"), 16)

        def step(n, par):
            if exists(n + 2):
                load_x(n + 2)
            if exists(n + 1):
                load_bias(n + 1, 0)
                load_mask(n + 1)
                stack(n + 1, 1 - par)
                for c in range(1, PIECES):
                    load_bias(n + 1, c)
            if exists(n - 1):
                sp.wait_ge(sem("result_ready"), n)
                sp.dma_start(out_rows[bass.ds(n - 1, 1)].rearrange("b p j d -> p (b j) d"), result[:]).then_inc(sem("out_sent"), 16)

        entries(sp, step)
        sp.wait_ge(sem("out_sent"), 16 * B)

    @block.gpsimd
    def _(pool):
        pool.memset(minus_half[:], -0.5).then_inc(sem("half_set2"), 1)
        for i in range(2):
            pool.memset(v_pad[i][:], 0.0).then_inc(sem("v_zeroed"), 1)
        pool.wait_ge(sem("half_set2"), 1)

        def rsqrt(out, var, ready, done, n):
            pool.wait_ge(sem(ready), n + 1)
            pool.tensor_tensor(out[:], var[:, :, 1], minus_half[:], ALU.pow).then_inc(sem(done), 1)

        def gather(n):
            wait_free(pool, sem("src_read"), n)
            wait_free(pool, sem("xmT_ready"), C * n)
            pool.tensor_copy(gate_now[:], gates[:, bass.ds(n, 1), :, :].rearrange("p b k j -> p (b k j)")).then_inc(sem("entry_cols"), 1)
            pool.tensor_copy(mod_now[:, 0, :], scale[:, :, bass.ds(n, 1)].rearrange("p c b -> p (c b)")).then_inc(sem("entry_cols"), 1)
            pool.tensor_copy(mod_now[:, 1, :], shift[:, :, bass.ds(n, 1)].rearrange("p c b -> p (c b)")).then_inc(sem("entry_cols"), 1)
            pool.tensor_copy(row_now[:], out_row[:, bass.ds(n, 1), :].rearrange("p b q -> p (b q)")).then_inc(sem("entry_cols"), 1)
            wait_alone(pool, sem("entry_cols"), 4 * (n + 1))
            for q in range(K * J):
                pool.indirect_dma_start(picked_rows[:, q, :], None, io["expert_out"],
                                        bass.IndirectOffsetOnAxis(ap=row_now[:, q:q + 1], axis=0),
                                        bounds_check=TILES * P - 1, oob_is_err=False).then_inc(sem("rows_in"), 16)

        def add_mask(n, c):
            pool.wait_ge(sem(f"bias_in{c}"), 16 * (n + 1))
            pool.wait_ge(sem("mask_taken"), n + 1)
            pool.tensor_tensor(bias[:, c, :, :], bias[:, c, :, :],
                               spread(mask_f[:].rearrange("p j k -> p (j k)"), [P, CHUNK, J * T], 1), ALU.add
                               ).then_inc(sem("bias_masked"), 1)

        def take_mask(n):
            wait_alone(pool, sem("mask_in"), 16 * (n + 1))
            wait_free(pool, sem("bias_masked"), PIECES * n, alone=True)
            pool.tensor_scalar(mask_f[:], mask[:].bitcast(U8), MASKED, None, ALU.mult).then_inc(sem("mask_taken"), 1)

        def step(n, par):
            if exists(n - 1):
                rsqrt(rstd2, mv2, "var2_ready", "rstd2_ready", n - 1)
            if exists(n):
                add_mask(n, PIECES - 1)
            if exists(n + 2):
                gather(n + 2)
            if exists(n + 1):
                take_mask(n + 1)
                for c in range(PIECES - 1):
                    add_mask(n + 1, c)
            if exists(n + 2):
                rsqrt(rstd, mv, "var_ready", "rstd_ready", n + 2)

        entries(pool, step)

    @block.scalar
    def _(act):
        for dst, name in ((wq, "wq"), (wk, "wk"), (wv, "wv"), (wo, "wo"), (w1, "ff_w1"), (w2, "ff_w2")):
            act.dma_start(dst[:], io[name]).then_inc(sem("layer_in"), 16)
        for i, dst in enumerate((bv, bo, b2)):
            act.dma_start(dst[:], io["rows"][i].partition_broadcast(P)).then_inc(sem("layer_in"), 16)

        def exponentials(n, h, par):
            act.wait_ge(sem("neg_ready"), J * (H * n + h + 1))
            wait_free(act, sem("p_turned"), H * n + h - 3)
            for j in range(J):
                act.activation(prob[h % 4][:, j, :], neg[h % 2][:, j, :], ACT.Exp, scale=-1.0,
                               bias=neg_max[par][:, h, j:j + 1], accum_out=total[par][:, h, j:j + 1]).then_inc(sem("p_ready"), 1)

        def take_probT(n, h):
            act.wait_ge(sem("p_turned"), H * n + h + 1)
            wait_free(act, sem("pv_done"), H * n + h - 3)
            act.activation(probT[h % 4][:], halves(ps_p[h % 2][:, :]), ACT.Copy).then_inc(sem("pT_scalar"), 1)

        def modulate(n, par):
            act.wait_ge(sem("xnT2_done"), n + 1)
            act.wait_ge(sem("entry_cols"), 4 * (n + 1))
            wait_free(act, sem("wo_done"), n - 1)
            for c in range(C):
                act.activation(xmT[par][:, c, :], ps_g[0][:, c * T:(c + 1) * T], ACT.Identity, bias=mod_now[:, 1, c:c + 1],
                               scale=mod_now[:, 0, c:c + 1]).then_inc(sem("xmT_ready"), 1)

        def upper(n, which, g, shift_by):
            act.wait_ge(sem(f"{which}_done"), n + 1)
            wait_free(act, sem("split_sent"), 64 * n)
            for m in range(C):
                act.activation(part[f"{which}_hi"][:, m, :], ps_g[g][:, m * T:(m + 1) * T], ACT.Identity,
                               bias=shift_by[:, m:m + 1]).then_inc(sem(f"{which}_split"), 1)

        def take_ctx(n, g):
            act.wait_ge(sem("pv_done"), H * n + (g + 1) * (H // 2))
            wait_free(act, sem("ctxT_ready"), n)
            act.activation(ctx_raw[:, g, :], ps_ctx[g][:, 0:T], ACT.Copy).then_inc(sem("ctx_taken"), 1)

        def take_hT(n):
            act.wait_ge(sem("h_turned"), n + 1)
            wait_free(act, sem("ff1_done"), 4 * n)
            for c in range(C):
                act.activation(hT[:, c, :], ps_g[1][:, c * T:(c + 1) * T], ACT.Identity, bias=vec[:, LN2_B + c:LN2_B + c + 1],
                               scale=vec[:, LN2_G + c:LN2_G + c + 1]).then_inc(sem("hT2_ready"), 1)

        def tanh(n, pair):
            act.wait_ge(sem("ff1_done"), 4 * n + pair + 1)
            wait_free(act, sem("act_ready"), F * n + 2 * (pair - 1))
            for i in range(2):
                f = 2 * pair + i
                act.activation(tanh_f[:, f % 4, :], ps_g[pair % 2][:, i * T:(i + 1) * T], ACT.Tanh, bias=tanh_b[:, f:f + 1],
                               scale=0.851).then_inc(sem("tanh2_ready"), 1)

        def step(n, par):
            for h in range(H):
                ahead, head = neighbour(n, h, 1)
                if exists(ahead):
                    exponentials(ahead, head, par if head else 1 - par)
                if exists(n) and by_scalar(h):
                    take_probT(n, h)
                if h == 0 and exists(n - 1):
                    take_ctx(n - 1, 1)
                if h == 8 and exists(n):
                    take_ctx(n, 0)
                if exists(n + 1):
                    if h == 2:
                        modulate(n + 1, 1 - par)
                    if h == 4:
                        upper(n + 1, "q", 0, q_b)
                    if h == 5:
                        upper(n + 1, "k", 1, vec[:, K_B:K_B + C])
                if exists(n - 1):
                    if h == 6:
                        take_hT(n - 1)
                    if 7 <= h < 11:
                        tanh(n - 1, h - 7)

        act.wait_ge(sem("setup_done"), 1)
        entries(act, step)

    @block.tensor
    def _(pe):
        def scores(n, h, par):
            if h == 0:
                wait_alone(pe, sem("stack_in"), 256 * (n + 1))
            wait_free(pe, sem("neg_ready"), J * (H * n + h - 1), alone=True)
            rows = slice((h % 2) * 64, (h % 2) * 64 + 64)
            for j in range(J):
                last = pe.matmul(ps_s[h % 2][:, j * T:(j + 1) * T], q_stack[par][rows, h // 2, j * P:(j + 1) * P].bitcast(F32R),
                                 k_stack[par][rows, h // 2, :].bitcast(F32R), start=True, stop=True)
            last.then_inc(sem("scores_done"), 1)

        def turn_probs(n, h):
            pe.wait_ge(sem("p_ready"), J * (H * n + h + 1))
            before, head = neighbour(n, h, -2)
            if exists(before):
                wait_probT(pe, before, head)
            for kt in range(J):
                for j in range(J):
                    last = pe.transpose(ps_p[h % 2][:, kt * T + j * P:kt * T + (j + 1) * P], prob[h % 4][:, j, kt * P:(kt + 1) * P], ident)
            last.then_inc(sem("p_turned"), 1)

        def weigh(n, h, par):
            wait_probT(pe, n, h)
            g, i = h // (H // 2), h % (H // 2)
            if h == 0:
                pe.wait_ge(sem("v_ready"), J * (n + 1))
            if i == 0:
                wait_free(pe, sem("ctx_taken"), C * n + g - 1)
            for kt in range(J):
                last = pe.matmul(ps_ctx[g][:, 0:T], v_pad[par][:, kt, g, i * P:(i + 1) * P], probT[h % 4][:, kt, :],
                                 start=(i == 0 and kt == 0), stop=(i == H // 2 - 1 and kt == J - 1))
            last.then_inc(sem("pv_done"), 1)

        def wait_probT(eng, n, h):
            if by_scalar(h):
                eng.wait_ge(sem("pT_scalar"), 12 * n + h - h // 4 + 1)
            else:
                eng.wait_ge(sem("pT_vector"), 4 * n + h // 4 + 1)

        def turn_inv(n):
            pe.wait_ge(sem("inv_ready"), n + 1)
            wait_free(pe, sem("result_ready"), n)
            for j in range(J):
                last = pe.transpose(ps_g[0][0:H, j * P:(j + 1) * P], inv[:, j, :], ident)
            last.then_inc(sem("inv_turned"), 1)

        def spread_inv(n):
            wait_alone(pe, sem("invT_ready"), n + 1)
            wait_free(pe, sem("act_ready"), F * n, alone=True)
            for m in range(C):
                last = pe.matmul(ps_g[1][:, m * T:(m + 1) * T], const[0:H, SPREAD + m * P:SPREAD + (m + 1) * P], invT[:, :],
                                 start=True, stop=True)
            last.then_inc(sem("inv_spread"), 1)

        def turn_x(n):
            pe.wait_ge(sem("xn2_ready"), J * (n + 1))
            wait_free(pe, sem("invT_ready"), n - 1)
            for c in range(C):
                for j in range(J):
                    last = pe.transpose(ps_g[0][:, c * T + j * P:c * T + (j + 1) * P], xn[:, j, c * P:(c + 1) * P], ident)
            last.then_inc(sem("xnT2_done"), 1)

        def output(n, par):
            pe.wait_ge(sem("ctxT_ready"), n + 1)
            for j in range(J):
                for m in range(C):
                    sums = ps_g[1][:, j * D + m * P:j * D + (m + 1) * P]
                    for c in range(C):
                        pe.matmul(sums, ctxT[:, c, j * P:(j + 1) * P], wo[:, c, m * P:(m + 1) * P], start=(c == 0), stop=False)
                    last = pe.matmul(sums, xmT[par][:, m, j * P:(j + 1) * P], ident, start=False, stop=True)
            last.then_inc(sem("wo_done"), 1)

        def query_or_key(n, par, which, w, g):
            if which == "q":
                pe.wait_ge(sem("xmT_ready"), C * (n + 1))
            else:
                wait_free(pe, sem("x3_ready"), n - 1)
            for m in range(C):
                for c in range(C):
                    last = pe.matmul(ps_g[g][:, m * T:(m + 1) * T], w[:, c, m * P:(m + 1) * P], xmT[par][:, c, :],
                                     start=(c == 0), stop=(c == C - 1))
            last.then_inc(sem(f"{which}_done"), 1)

        def values(n, par):
            pe.wait_ge(sem("q_split"), 2 * C * (n + 1))
            for kt in range(J):
                for c in range(C):
                    last = pe.matmul(ps_g[0][:, kt * D:(kt + 1) * D], xmT[par][:, c, kt * P:(kt + 1) * P], wv[:, c, :],
                                     start=(c == 0), stop=(c == C - 1))
            last.then_inc(sem("v_done"), 1)

        def turn_h(n):
            pe.wait_ge(sem("h_rows_ready"), J * (n + 1))
            if exists(n + 2):
                pe.wait_ge(sem("k_split"), 2 * C * (n + 3))
            for c in range(C):
                for j in range(J):
                    last = pe.transpose(ps_g[1][:, c * T + j * P:c * T + (j + 1) * P], h_rows[:, j, c * P:(c + 1) * P], ident)
            last.then_inc(sem("h_turned"), 1)

        def feed_up(n, pair):
            if pair == 0:
                pe.wait_ge(sem("hT2_ready"), C * (n + 1))
                if exists(n + 2):
                    pe.wait_ge(sem("v_ready"), J * (n + 3))
            elif pair >= 2:
                pe.wait_ge(sem("act_ready"), F * n + 2 * (pair - 1))
            for i in range(2):
                f = 2 * pair + i
                for c in range(C):
                    last = pe.matmul(ps_g[pair % 2][:, i * T:(i + 1) * T], w1[:, c, f * P:(f + 1) * P], hT[:, c, :],
                                     start=(c == 0), stop=(c == C - 1))
            last.then_inc(sem("ff1_done"), 1)

        def feed_down(n, quarter):
            j, half = quarter // 2, quarter % 2
            pe.wait_ge(sem("act_ready"), F * n + (F if quarter else F // 2 + 2))
            for f in range(4 * half, 4 * half + 4):
                last = pe.matmul(ps_g[0][:, j * D:(j + 1) * D], act_f[:, f, j * P:(j + 1) * P], w2[:, f, :],
                                 start=(f == 0), stop=(f == F - 1))
            if quarter == 3:
                last.then_inc(sem("ff2_done"), 1)

        def step(n, par):
            for h in range(H):
                ahead, head = neighbour(n, h, 2)
                if exists(ahead):
                    scores(ahead, head, par if head >= 2 else 1 - par)
                if exists(n):
                    turn_probs(n, h)
                if exists(n - 1):
                    if h == 0:
                        turn_inv(n - 1)
                    if h == 1:
                        spread_inv(n - 1)
                    if h == 3:
                        output(n - 1, 1 - par)
                if exists(n + 1):
                    if h == 2:
                        turn_x(n + 1)
                    if h == 4:
                        query_or_key(n + 1, 1 - par, "q", wq, 0)
                    if h == 5:
                        query_or_key(n + 1, 1 - par, "k", wk, 1)
                    if h == 6:
                        values(n + 1, 1 - par)
                if exists(n - 1):
                    if h == 6:
                        turn_h(n - 1)
                    if 7 <= h < 11:
                        feed_up(n - 1, h - 7)
                    if 11 <= h < 15:
                        feed_down(n - 1, h - 11)
                before, head = neighbour(n, h, -1)
                if exists(before):
                    weigh(before, head, par if head < H - 1 else 1 - par)

        pe.wait_ge(sem("setup_done"), 1)
        entries(pe, step)

    @block.vector
    def _(dve):
        def chain(name, count, n):
            return Steps(dve, sem(name), count * n)

        def combine_first(n):
            wait_free(dve, sem("xn2_ready"), J * n)
            dve.wait_ge(sem("x2_in"), 16 * (n + 1))
            dve.wait_ge(sem("rows_in"), 16 * K * J * (n + 1))
            dve.wait_ge(sem("entry_cols"), 4 * (n + 1))
            for j in range(J):
                last = dve.scalar_tensor_tensor(src[:, j, :], picked_rows[:, j, :], gate_now[:, j:j + 1], x[:, j, :], ALU.mult, ALU.add)
            last.then_inc(sem("src_started"), 1)

        def combine_second(n):
            dve.wait_ge(sem("src_started"), n + 1)
            for j in range(J):
                last = dve.scalar_tensor_tensor(src[:, j, :], picked_rows[:, J + j, :], gate_now[:, J + j:J + j + 1], src[:, j, :],
                                                ALU.mult, ALU.add)
            last.then_inc(sem("src_read"), 1)

        def input_moments(n):
            s = chain("src_step", 2, n)
            wait_alone(dve, sem("src_read"), n + 1)
            for j in range(J):
                last = dve.bn_stats(stats[:, j, :], src[:, j, :])
            s.then_alone(last)
            for j in range(J):
                last = dve.bn_aggr(mv[:, j, :], stats[:, j, :])
            s.then(last)
            dve.tensor_scalar(mv[:, :, 1], mv[:, :, 1], 1e-5, None, ALU.add).then_inc(sem("var_ready"), 1)

        def normalise(n):
            dve.wait_ge(sem("rstd_ready"), n + 1)
            for j in range(J):
                dve.tensor_scalar(xn[:, j, :], src[:, j, :], mv[:, j, 0:1], rstd[:, j:j + 1],
                                  ALU.subtract, ALU.mult).then_inc(sem("xn2_ready"), 1)

        def minimum(n, h, par):
            wait_alone(dve, sem("scores_done"), H * n + h + 1)
            if h % CHUNK == 0:
                wait_alone(dve, sem("bias_masked"), PIECES * n + h // CHUNK + 1)
            wait_free(dve, sem("p_ready"), J * (H * n + h - 1), alone=True)
            for j in range(J):
                dve.tensor_tensor_reduce(neg[h % 2][:, j, :], ps_s[h % 2][:, j * T:(j + 1) * T],
                                         bias[:, h // CHUNK, h % CHUNK, j * T:(j + 1) * T], -1.0, -MASKED,
                                         ALU.add, ALU.min, neg_max[par][:, h, j:j + 1]).then_inc(sem("neg_ready"), 1)

        def take_probT(n, h):
            dve.wait_ge(sem("p_turned"), H * n + h + 1)
            wait_free(dve, sem("pv_done"), H * n + h - 3)
            dve.tensor_copy(probT[h % 4][:], halves(ps_p[h % 2][:, :])).then_inc(sem("pT_vector"), 1)

        def inverse(n, par):
            s = chain("inv_step", 2, n)
            dve.wait_ge(sem("p_ready"), J * H * (n + 1))
            wait_free(dve, sem("inv_turned"), n)
            s.did(dve.tensor_scalar(undefined[:], neg_max[par][:], 1e10, 0.0, ALU.mult, ALU.mult))
            s.then(dve.reciprocal(inv[:].rearrange("p j h -> p h j"), total[par][:]))
            dve.tensor_tensor(inv[:], inv[:], undefined[:].rearrange("p h j -> p j h"), ALU.add).then_inc(sem("inv_ready"), 1)

        def take_inv(n):
            dve.wait_ge(sem("inv_turned"), n + 1)
            wait_free(dve, sem("inv_spread"), n)
            dve.tensor_copy(invT[:], ps_g[0][0:H, 0:T]).then_inc(sem("invT_ready"), 1)

        def scale_ctx(n):
            dve.wait_ge(sem("inv_spread"), n + 1)
            dve.wait_ge(sem("ctx_taken"), C * (n + 1))
            wait_free(dve, sem("wo_done"), n)
            dve.tensor_tensor(ctxT[:], ctx_raw[:], halves(ps_g[1][:, :]), ALU.mult).then_inc(sem("ctxT_ready"), 1)

        def lower(n, which, g, shift_by):
            dve.wait_ge(sem(f"{which}_split"), C * (2 * n + 1))
            for m in range(C):
                dve.scalar_tensor_tensor(part[f"{which}_lo"][:, m, :], ps_g[g][:, m * T:(m + 1) * T], shift_by[:, m:m + 1],
                                         part[f"{which}_hi"][:, m, :].bitcast(F32), ALU.add, ALU.subtract).then_inc(sem(f"{which}_split"), 1)

        def take_values(n, par):
            dve.wait_ge(sem("v_done"), n + 1)
            if n_int_or(n) >= 2:
                dve.wait_ge(sem("pv_done"), H * (n - 1))
            for kt in range(J):
                dve.tensor_tensor(v_pad[par][:, kt, :, :].rearrange("p g (i w) -> p g i w", w=P + HD)[:, :, :, 0:HD],
                                  ps_g[0][:, kt * D:(kt + 1) * D].rearrange("p (g i w) -> p g i w", g=C, w=HD),
                                  bv[:].rearrange("p (g i w) -> p g i w", g=C, w=HD), ALU.add).then_inc(sem("v_ready"), 1)

        def residual(n):
            dve.wait_ge(sem("wo_done"), n + 1)
            wait_free(dve, sem("h_rows_ready"), J * n)
            dve.tensor_tensor(x3[:], halves(ps_g[1][:, :]), spread(bo[:], [P, J, D], 1), ALU.add).then_inc(sem("x3_ready"), 1)

        def moments(n):
            s = chain("ln2_step", 2, n)
            wait_alone(dve, sem("x3_ready"), n + 1)
            for j in range(J):
                last = dve.bn_stats(stats2[:, j, :], x3[:, j, :])
            s.then_alone(last)
            wait_free(dve, sem("rstd2_ready"), n, alone=True)
            for j in range(J):
                last = dve.bn_aggr(mv2[:, j, :], stats2[:, j, :])
            s.then(last)
            dve.tensor_scalar(mv2[:, :, 1], mv2[:, :, 1], 1e-5, None, ALU.add).then_inc(sem("var2_ready"), 1)

        def prepare_sum(n):
            wait_free(dve, sem("result_ready"), n)
            dve.tensor_tensor(x3b[:], x3[:], spread(b2[:], [P, J, D], 1), ALU.add).then_inc(sem("x3b_ready"), 1)

        def normalise2(n):
            dve.wait_ge(sem("rstd2_ready"), n + 1)
            wait_free(dve, sem("h_turned"), n)
            for j in range(J):
                dve.tensor_scalar(h_rows[:, j, :], x3[:, j, :], mv2[:, j, 0:1], rstd2[:, j:j + 1],
                                  ALU.subtract, ALU.mult).then_inc(sem("h_rows_ready"), 1)

        def gelu(n, pair):
            dve.wait_ge(sem("tanh2_ready"), F * n + 2 * pair + 2)
            wait_free(dve, sem("act_ready"), F * n + 2 * (pair - 1))
            for i in range(2):
                f = 2 * pair + i
                dve.tensor_scalar(up_f[:, f % 4, :], ps_g[pair % 2][:, i * T:(i + 1) * T], vec[:, FF_B1 + f:FF_B1 + f + 1], None,
                                  ALU.add).then_inc(sem("up_ready"), 1)
            dve.wait_ge(sem("up_ready"), F * n + 2 * pair + 2)
            if pair == 0:
                wait_free(dve, sem("ff2_done"), n)
            for i in range(2):
                f = 2 * pair + i
                dve.scalar_tensor_tensor(act_f[:, f, :], tanh_f[:, f % 4, :], 1.0, up_f[:, f % 4, :], ALU.add, ALU.mult).then_inc(sem("act_ready"), 1)

        def finish(n):
            dve.wait_ge(sem("ff2_done"), n + 1)
            dve.wait_ge(sem("x3b_ready"), n + 1)
            wait_free(dve, sem("out_sent"), 16 * n)
            dve.tensor_tensor(result[:], halves(ps_g[0][:, :]), x3b[:], ALU.add).then_inc(sem("result_ready"), 1)

        def step(n, par):
            for h in range(H):
                ahead, head = neighbour(n, h, 1)
                if exists(ahead):
                    minimum(ahead, head, par if head else 1 - par)
                if exists(n) and not by_scalar(h):
                    take_probT(n, h)
                if exists(n - 1):
                    if h == 0:
                        take_inv(n - 1)
                    if h == 1:
                        scale_ctx(n - 1)
                    if h == 3:
                        residual(n - 1)
                    if h == 4:
                        moments(n - 1)
                    if h == 5:
                        normalise2(n - 1)
                    if 8 <= h < 12:
                        gelu(n - 1, h - 8)
                    if h == 12:
                        prepare_sum(n - 1)
                    if h == 15:
                        finish(n - 1)
                if exists(n + 1):
                    if h == 0:
                        normalise(n + 1)
                    if h == 5:
                        lower(n + 1, "q", 0, q_b)
                    if h == 6:
                        lower(n + 1, "k", 1, vec[:, K_B:K_B + C])
                        take_values(n + 1, 1 - par)
                if exists(n + 2):
                    if h == 12:
                        combine_first(n + 2)
                    if h == 13:
                        combine_second(n + 2)
                    if h == 14:
                        input_moments(n + 2)
                if h == H - 1 and exists(n):
                    inverse(n, par)

        dve.wait_ge(sem("layer_in"), 16 * 9)
        dve.wait_ge(sem("v_zeroed"), 2)
        dve.tensor_scalar(wq[:], wq[:], 1.0 / 4, None, ALU.mult)
        dve.tensor_scalar(w2[:], w2[:], 0.5, None, ALU.mult)
        dve.tensor_scalar(q_b[:], vec[:, Q_B:Q_B + C], 1.0 / 4, None, ALU.mult)
        dve.tensor_scalar(tanh_b[:], vec[:, FF_B1:FF_B1 + F], 0.851, None, ALU.mult).then_inc(sem("setup_done"), 1)
        dve.wait_ge(sem("setup_done"), 1)
        entries(dve, step)


def n_int_or(n):
    return n if isinstance(n, int) else B


def layers(nc, io):
    with ExitStack() as ctx:
        keep = {
            "const": ctx.enter_context(nc.sbuf_tensor("const", [P, CONSTS], F32)),
            "vec": ctx.enter_context(nc.sbuf_tensor("vec", [P, VECS], F32)),
            "gates": ctx.enter_context(nc.sbuf_tensor("gates", [P, B, K, J], F32)),
            "out_row": ctx.enter_context(nc.sbuf_tensor("out_row", [P, B, K * J], U32)),
            "scale": ctx.enter_context(nc.sbuf_tensor("scale", [P, C, B], F32)),
            "shift": ctx.enter_context(nc.sbuf_tensor("shift", [P, C, B], F32)),
            "xn": ctx.enter_context(nc.sbuf_tensor("xn", [P, J, D], F32)),
            "consts_in": ctx.enter_context(nc.semaphore("consts_in")),
        }
        io["dispatch"] = nc.dram_tensor("dispatch", (E * REGION, D), F32, kind="Internal").ap()
        io["expert_out"] = nc.dram_tensor("expert_out", (TILES * P, D), F32, kind="Internal").ap()
        for name in ("q_hi", "q_lo", "k_hi", "k_lo"):
            io[name] = nc.dram_tensor(name + "_rows", (D, T), F32, kind="Internal").ap()
        with ExitStack() as first:
            condition_and_route(nc, first, io, keep)
        with ExitStack() as second:
            transformer(nc, second, io, keep)


def kernel(**inputs):
    import concourse.bacc as bacc
    from concourse.bass_utils import run_bass_kernel_spmd

    given = {k: np.asarray(v) for k, v in inputs.items()}

    def first(name):
        return given["L0_cond_" + name]

    def second(name):
        return given["L1_cond_" + name]

    def columns(v):
        return np.pad(v, (0, -len(v) % P)).reshape(-1, P).T

    def chunks(w):
        return np.ascontiguousarray(w.reshape(-1, P, w.shape[-1]).transpose(1, 0, 2))

    freq = np.exp(np.arange(D // 2, dtype=np.float32) * np.float32(-np.log(10000.0) / (D // 2 - 1))).astype(np.float32)
    const = np.zeros((P, CONSTS), np.float32)
    const[:, IDENT:IDENT + P] = np.eye(P)
    const[:, BELOW:BELOW + P] = np.triu(np.ones((P, P)), 1)
    const[:, ONES:ONES + P] = 1
    const[:, SLOT:SLOT + E] = np.arange(E)
    const[:, TILE_NO:TILE_NO + TILES] = np.arange(TILES)
    const[:, REGION_ROW:REGION_ROW + E] = np.arange(E) * REGION
    const[0:H, SPREAD:SPREAD + D] = np.kron(np.eye(H), np.ones((1, HD)))

    vec = np.concatenate([columns(first(n)) for n in ("ln_g", "ln_b", "hyp_b1", "hyp_b2", "sty_b1", "sty_b2")]
                         + [columns(second(n)) for n in ("b_ada", "bq", "bk", "b1", "g2", "beta2")]
                         + [columns(freq), columns(np.arange(P, dtype=np.float32))], axis=1).astype(np.float32)

    arrays = {
        "x": given["x"].reshape(B * T, D),
        "subject": given["itok_B_6_14"].reshape(B, 1).view(np.uint32),
        "timestep": given["itok_B_34_63"],
        "bias": given["fside_Bx16xSxS_0"],
        "mask": given["mask_Bx1xSxS_bk0"].reshape(B, T, T).view(np.uint32),
        "vec": vec, "const": const,
        "subj_emb": first("subj_emb"), "hyp_w1": first("hyp_w1"), "hyp_w2": first("hyp_w2"),
        "sty_w1": first("sty_w1"), "sty_w2": first("sty_w2"),
        "ada_w": chunks(second("W_ada")), "router": chunks(first("router_w")),
        "w1": first("exp_w1").reshape(E, C, P, FF).transpose(2, 0, 1, 3).reshape(P, E, C * FF),
        "w2": first("exp_w2").reshape(E, F, P, D).transpose(2, 0, 1, 3).reshape(P, E, F * D),
        "b1": first("exp_b1"), "b2": first("exp_b2"),
        "wq": chunks(second("Wq")), "wk": chunks(second("Wk")), "wv": chunks(second("Wv")), "wo": chunks(second("Wo")),
        "ff_w1": chunks(second("W1")), "ff_w2": chunks(second("W2")),
        "rows": np.stack([second("bv"), second("bo"), second("b2")]),
    }
    arrays = {k: np.ascontiguousarray(v) for k, v in arrays.items()}

    nc = bacc.Bacc("TRN2", target_bir_lowering=False, num_devices=1)
    io = {k: nc.dram_tensor(k + "_dram", v.shape, mybir.dt.from_np(v.dtype), kind="ExternalInput").ap() for k, v in arrays.items()}
    io["out"] = nc.dram_tensor("out_dram", (B * T, D), F32, kind="ExternalOutput").ap()
    layers(nc, io)
    result = run_bass_kernel_spmd(nc, [{k + "_dram": v for k, v in arrays.items()}], core_ids=[0])
    return result.results[0]["out_dram"].reshape(B, T, D)
```

```python
from contextlib import ExitStack

import numpy as np

import concourse.bass as bass
from concourse import mybir

F32 = mybir.dt.float32
F32R = mybir.dt.float32r
I32 = mybir.dt.int32
U32 = mybir.dt.uint32
U8 = mybir.dt.uint8
ALU = mybir.AluOpType
ACT = mybir.ActivationFunctionType
X = mybir.AxisListType.X

P = 128
B, T, D = 16, 256, 256
J = T // P
C = D // P
E, FF = 8, 1024
F = FF // P
K = 2
H, HD = 16, 16
SUBJ, SE, SH = 32, 64, 128
REGION = B * T + P
TILES = (K * B * T - P) // P + E
MAGIC = 8388608.0
MASKED = -3.0e38

LN_G, LN_B, HYP_B1, HYP_B2, STY_B1, STY_B2 = 0, 2, 4, 5, 6, 7
ADA_B, Q_B, K_B, FF_B1, LN2_G, LN2_B = 11, 15, 17, 19, 27, 29
FREQ, PART, VECS = 31, 32, 33
IDENT, BELOW, ONES, SLOT, TILE_NO, REGION_ROW, SPREAD, CONSTS = 0, 128, 256, 384, 392, 464, 472, 728


class Steps:

    def __init__(self, eng, sem, base=0):
        self.eng, self.sem, self.at = eng, sem, base

    def did(self, instruction):
        self.at = self.at + 1
        instruction.then_inc(self.sem, 1)

    def then(self, instruction):
        self.did(instruction)
        self.eng.wait_ge(self.sem, self.at)

    def then_alone(self, instruction):
        self.did(instruction)
        wait_alone(self.eng, self.sem, self.at)


def wait_alone(eng, sem, value):
    if isinstance(value, int):
        eng.wait_ge(sem, value)
    else:
        value = eng.to_reg(value)
        eng.wait_ge(sem, 1)
        eng.wait_ge(sem, value)


def wait_free(eng, sem, value, alone=False):
    if isinstance(value, int):
        if value > 0:
            eng.wait_ge(sem, value)
    elif alone:
        wait_alone(eng, sem, value)
    else:
        eng.wait_ge(sem, value)


def exists(n):
    return not isinstance(n, int) or 0 <= n < B


def neighbour(n, h, ahead):
    h = h + ahead
    return (n + h // H if h // H else n), h % H


def entries(eng, step):
    for n in range(-2, 3):
        step(n, n % 2)
    with eng.Fori(1, B // 2 - 2) as i:
        step(2 * i + 1, 1)
        step(2 * i + 2, 0)
    for n in range(B - 3, B + 2):
        step(n, n % 2)


def spread(ap, shape, at):
    return ap.unsqueeze(at).to_broadcast(shape)


def condition_and_route(nc, ctx, io, keep):
    sems = {}

    def sem(name):
        if name not in sems:
            sems[name] = ctx.enter_context(nc.semaphore(name))
        return sems[name]

    def sb(name, shape, dt=F32):
        return ctx.enter_context(nc.sbuf_tensor(name, shape, dt))

    def bank(name):
        return ctx.enter_context(nc.psum_tensor(name, [P, 512], F32))

    const, vec = keep["const"], keep["vec"]
    ident = const[:, IDENT:IDENT + P]
    below = const[:, BELOW:BELOW + P]
    ones = const[:, ONES:ONES + P]
    slot8 = const[:, SLOT:SLOT + E]
    region_row = const[:, REGION_ROW:REGION_ROW + E]
    gates, out_row = keep["gates"], keep["out_row"]

    w1 = sb("w1", [P, E, C * FF])
    w2 = sb("w2", [P, E, F * D])
    router = sb("router", [P, C, E])
    zeros = sb("zeros", [P, D])

    xin = [sb(f"xin{i}", [P, J, D]) for i in range(2)]
    row_stats = sb("row_stats", [P, J, 6])
    row_mv = sb("row_mv", [P, J, 2])
    row_rstd = sb("row_rstd", [P, J])
    col_stats = sb("col_stats", [P, C, 6])
    col_mv = sb("col_mv", [P, C, 2])
    col_rstd = sb("col_rstd", [P, C])
    col_scale = sb("col_scale", [P, C])
    col_mean_s = sb("col_mean_s", [P, C])
    col_shift = sb("col_shift", [P, C])
    minus_half = sb("minus_half", [P, 2])
    gamma = sb("gamma", [P, C, B])
    beta = sb("beta", [P, C, B])
    columns = sb("columns", [P, 2, C * T])
    hT, h2T = [columns[:, i, :].rearrange("p (c t) -> p c t", c=C) for i in range(2)]
    token_rows = sb("token_rows", [P, 2, J * D])
    h2 = [token_rows[:, i, :].rearrange("p (j d) -> p j d", j=J) for i in range(2)]
    logits = sb("logits", [P, J, E])
    best = sb("best", [P, J, E])
    best_at = sb("best_at", [P, J, E], U32)
    gap = sb("gap", [P, J])
    gap_exp = sb("gap_exp", [P, J])
    gap_sum = sb("gap_sum", [P, J])
    chosen = sb("chosen", [P, K, J])
    onehot = sb("onehot", [P, K * J, E])
    picked = sb("picked", [P, J, E])
    count = sb("count", [P, E])
    rank_base = sb("rank_base", [P, J, E])
    count_mid = sb("count_mid", [P, E])
    rank_sel = sb("rank_sel", [P, K * J, E])
    row_f = sb("row_f", [P, K * J])
    row_i = [sb(f"row_i{i}", [P, K * J], U32) for i in range(2)]
    chosen_all = sb("chosen_all", [P, B, K * J])
    row_all = sb("row_all", [P, B, K * J])
    tiles_n = sb("tiles_n", [P, E])
    tiles_cum = [sb(f"tiles_cum{i}", [P, E]) for i in range(2)]
    delta = sb("delta", [P, E])
    pad_f = sb("pad_f", [P, E])
    pad_i = sb("pad_i", [P, E], U32)
    tile_e = sb("tile_e", [1, TILES])
    tile_ok = sb("tile_ok", [1, TILES])
    tile_row = sb("tile_row", [1, TILES])
    tile_tab = sb("tile_tab", [1, 2, TILES], I32)
    htok = [xin[0][:, i, :] for i in range(2)]
    y = xin[1][:, 0, :]
    hid = token_rows[:].rearrange("p i n -> p (i n)")
    htokT = {n: sb(f"htokT_{n}", [P, C, P], F32R) for n in ("hi", "lo")}
    hidT = {n: sb(f"hidT_{n}", [P, FF], F32R) for n in ("hi", "lo")}
    w1_part = {n: sb(f"w1_{n}", [P, PARTS, 512], F32R) for n in ("hi", "lo")}
    w2_part = {n: sb(f"w2_{n}", [P, PARTS, 512], F32R) for n in ("hi", "lo")}
    b1 = [sb(f"b1_row{i}", [P, FF]) for i in range(2)]
    b2 = [sb(f"b2_row{i}", [P, D]) for i in range(2)]
    big = columns[:, 0, :].rearrange("p (q e) -> p q e", e=E)
    tiles = b1[1][0:1, 0:TILES * E].rearrange("p (t e) -> p t e", e=E)
    ada_w = b1[0][:].rearrange("p (c n) -> p c n", c=C)
    sty_w2 = b1[1][0:SH // 2, 0:2 * D]

    ps_t, ps_h0, ps_h1, ps_th0, ps_th1, ps_y = [bank(n) for n in ("ps_t", "ps_h0", "ps_h1", "ps_th0", "ps_th1", "ps_y")]
    ps_logit, ps_rank, ps_back = ps_th0, ps_th1, ps_y
    ps_h, ps_th = [ps_h0, ps_h1], [ps_th0, ps_th1]

    x_rows = io["x"].rearrange("(b j p) d -> b p j d", j=J, p=P)
    dispatch, expert_out = io["dispatch"], io["expert_out"]

    consts_in = keep["consts_in"]
    consts_need = 16 * 2
    cond = cond_weights(nc, sb, ada_w, sty_w2)

    def w1_piece(e, k):
        start = (k % C) * FF + (k // C) * 512
        return w1[:, bass.ds(e, 1), start:start + 512].rearrange("p e n -> p (e n)")

    def w2_piece(e, k):
        return w2[:, bass.ds(e, 1), k * 512:(k + 1) * 512].rearrange("p e n -> p (e n)")

    block = ctx.enter_context(nc.Block())

    @block.sync
    def _(sp):
        sp.dma_start(const[:], io["const"]).then_inc(consts_in, 16)
        sp.dma_start(vec[:], io["vec"]).then_inc(consts_in, 16)
        for i in range(2):
            sp.dma_start(xin[i][:], x_rows[i]).then_inc(sem(f"x_in{i}"), 16)
        sp.dma_start(cond["t_int"][:], io["timestep"].partition_broadcast(P)).then_inc(sem("cond_in"), 16)
        sp.dma_start(cond["ids"][:], io["subject"]).then_inc(sem("ids_in"), 16)
        sp.dma_start(cond["hyp_w1"][:], io["hyp_w1"]).then_inc(sem("cond_in"), 16)
        sp.dma_start(cond["hyp_w2"][:], io["hyp_w2"]).then_inc(sem("cond_in"), 16)
        sp.dma_start(cond["sty_w1"][:], io["sty_w1"]).then_inc(sem("cond_in"), 16)
        sp.dma_start(cond["sty_w2"], io["sty_w2"]).then_inc(sem("cond_in"), 16)
        sp.dma_start(cond["ada_w"], io["ada_w"]).then_inc(sem("cond_in"), 16)
        sp.dma_start(router[:], io["router"]).then_inc(sem("router_in"), 16)
        with sp.Fori(1, B // 2) as i:
            for par in range(2):
                wait_alone(sp, sem("xn_ready"), J * (2 * i + par - 1))
                sp.dma_start(xin[par][:], x_rows[bass.ds(2 * i + par, 1)].rearrange("b p j d -> p (b j) d")
                             ).then_inc(sem(f"x_in{par}"), 16)

        for par in range(2):
            sp.wait_ge(sem(f"row_sent{par}"), 16 * K * J * (B // 2))
        sp.wait_ge(sem("pad_sent"), 16 * E)
        sp.wait_ge(sem("tables_ready"), 1)

        def expert_of(t):
            return sp.value_load(tile_tab[0:1, 0, bass.ds(t, 1)], min_val=0, max_val=E - 1)

        def load(tile):
            wait_free(sp, sem("tile_turned"), tile.t - 1, alone=True)
            row = sp.value_load(tile_tab[0:1, 1, bass.ds(tile.t, 1)], min_val=0, max_val=E * REGION - P)
            sp.dma_start(htok[tile.par], dispatch[bass.ds(row, P), :]).then_inc(sem(f"tile_in{tile.par}"), 16)

        def load_b1(tile):
            wait_free(sp, sem("hid_ready"), 2 * (tile.t - 1), alone=True)
            row = io["b1"][bass.ds(expert_of(tile.t), 1), :].rearrange("e n -> (e n)")
            sp.dma_start(b1[tile.par][:], row.partition_broadcast(P)).then_inc(sem(f"b1_in{tile.par}"), 16)

        def load_b2(tile):
            wait_free(sp, sem("y_ready"), tile.t - 1, alone=True)
            row = io["b2"][bass.ds(expert_of(tile.t), 1), :].rearrange("e n -> (e n)")
            sp.dma_start(b2[tile.par][:], row.partition_broadcast(P)).then_inc(sem(f"b2_in{tile.par}"), 16)

        def store(t):
            sp.wait_ge(sem("y_ready"), t + 1)
            sp.dma_start(expert_out[bass.ds(t * P, P), :], y).then_inc(sem("y_sent"), 16)

        def body(tile):
            if a_tile(tile.t + 2):
                load(tile.ahead(2))
                load_b1(tile.ahead(2))
            if a_tile(tile.t - 1):
                store(tile.t - 1)
            if a_tile(tile.t + 1):
                load_b2(tile.ahead(1))

        load(Tile(0, 0))
        load_b1(Tile(0, 0))
        tile_loop(sp, body)
        sp.wait_ge(sem("y_sent"), 16 * TILES)

    @block.gpsimd
    def _(pool):
        pool.memset(minus_half[:], -0.5).then_inc(sem("half_set"), 1)
        pool.memset(zeros[:], 0.0).then_inc(sem("zeros_set"), 1)
        pool.wait_ge(sem("half_set"), 1)
        pool.wait_ge(sem("ids_in"), 16)
        pool.indirect_dma_start(cond["emb"][0:B, :], None, io["subj_emb"],
                                bass.IndirectOffsetOnAxis(ap=cond["ids"][:, 0:1], axis=0),
                                bounds_check=SUBJ - 1, oob_is_err=False).then_inc(sem("emb_in"), 16)

        def row_rsqrt(b):
            pool.wait_ge(sem("row_var_ready"), b + 1)
            if not (isinstance(b, int) and b == 0):
                pool.wait_ge(sem("xn_ready"), J * b)
            pool.tensor_tensor(row_rstd[:], row_mv[:, :, 1], minus_half[:, 0:J], ALU.pow).then_inc(sem("row_rstd_ready"), 1)

        def col_rsqrt(b):
            pool.wait_ge(sem("col_var_ready"), b + 1)
            pool.tensor_tensor(col_rstd[:], col_mv[:, :, 1], minus_half[:, 0:C], ALU.pow).then_inc(sem("col_rstd_ready"), 1)

        def send_rows(b, par):
            wait_alone(pool, sem("row_i_ready"), b + 1)
            wait_alone(pool, sem("h2_ready"), b + 1)
            for k in range(K):
                for j in range(J):
                    q = k * J + j
                    pool.indirect_dma_start(dispatch, bass.IndirectOffsetOnAxis(ap=row_i[par][:, q:q + 1], axis=0),
                                            h2[par][:, j, :], None,
                                            bounds_check=E * REGION - 1, oob_is_err=False).then_inc(sem(f"row_sent{par}"), 16)

        def step(i, par, rows, cols, routed):
            b = 2 * i + par
            if rows:
                row_rsqrt(b)
            if cols:
                col_rsqrt(b - 1)
            if routed:
                send_rows(b - 2, par)

        pipeline(pool, step)
        pool.wait_ge(sem("zeros_set"), 1)
        pool.wait_ge(sem("pad_ready"), 1)
        for e in range(E):
            pool.indirect_dma_start(dispatch, bass.IndirectOffsetOnAxis(ap=pad_i[:, e:e + 1], axis=0),
                                    zeros[:], None,
                                    bounds_check=E * REGION - 1, oob_is_err=False).then_inc(sem("pad_sent"), 16)

        pool.wait_ge(sem("tables_ready"), 1)

        def body(tile):
            if a_tile(tile.t):
                e = pool.value_load(tile_tab[0:1, 0, bass.ds(tile.t, 1)], min_val=0, max_val=E - 1)
                for k in range(PARTS):
                    wait_alone(pool, sem("w2_upper"), PARTS * tile.t + k + 1)
                    pool.tensor_tensor(w2_part["lo"][:, k, :], w2_piece(e, k), w2_part["hi"][:, k, :].bitcast(F32),
                                       ALU.subtract).then_inc(sem("w2_split"), 1)

        tile_loop(pool, body)

    @block.scalar
    def _(act):
        cond_scalar(nc, act, cond, vec, sem)

        def load_experts(b):
            for dst, src in ((w1, io["w1"]), (w2, io["w2"])):
                dst, src = [ap.rearrange("p e (i n) -> p (e i) n", i=2)[:, bass.ds(b, 1), :] for ap in (dst[:], src)]
                act.dma_start(dst, src).then_inc(sem("w_in"), 16)

        def step(i, par, rows, cols, routed):
            b = 2 * i + par
            if rows:
                load_experts(b)
            if routed:
                act.wait_ge(sem("gap_ready"), b - 1)
                act.activation(gap_exp[:], gap[:], ACT.Exp).then_inc(sem("gap_exp_ready"), 1)
            if rows:
                act.wait_ge(sem("xnT_done"), b + 1)
                if not (isinstance(b, int) and b == 0):
                    act.wait_ge(sem("h2T_ready"), b)
                for c in range(C):
                    act.activation(hT[:, c, :], ps_t[:, c * T:(c + 1) * T], ACT.Identity, bias=vec[:, LN_B + c:LN_B + c + 1],
                                   scale=vec[:, LN_G + c:LN_G + c + 1]).then_inc(sem("hT_ready"), 1)
            if cols:
                p = 1 - par
                own = i if par else i - 1
                act.wait_ge(sem("back_done"), b)
                if not (isinstance(own, int) and own == 0):
                    act.wait_ge(sem(f"row_sent{p}"), 16 * K * J * own)
                act.activation(h2[p], ps_back[:, :].rearrange("p (j d) -> p j d", j=J), ACT.Copy).then_inc(sem("h2_ready"), 1)

        pipeline(act, step)

        def take_in(t):
            act.wait_ge(sem("tile_turned"), t + 1)
            wait_free(act, sem("w1_used"), PARTS * t)
            act.activation(htokT["hi"][:], ps_t[:, 0:C * P].rearrange("p (c m) -> p c m", c=C), ACT.Copy).then_inc(sem("htokT_upper"), 1)

        def relu(t):
            act.wait_ge(sem("hid_turned"), t + 1)
            wait_free(act, sem("w2_used"), PARTS * t)
            for i in range(2):
                act.activation(hidT["hi"][:, i * 512:(i + 1) * 512], ps_th[i][:, :], ACT.Relu).then_inc(sem("hidT_upper"), 1)

        def upper_w1(t):
            e = act.value_load(tile_tab[0:1, 0, bass.ds(t, 1)], min_val=0, max_val=E - 1)
            for k in range(PARTS):
                wait_free(act, sem("w1_used"), PARTS * (t - 1) + k + 1, alone=True)
                act.activation(w1_part["hi"][:, k, :], w1_piece(e, k), ACT.Copy).then_inc(sem("w1_upper"), 1)

        def upper_w2(t):
            e = act.value_load(tile_tab[0:1, 0, bass.ds(t, 1)], min_val=0, max_val=E - 1)
            for k in range(PARTS):
                wait_free(act, sem("w2_used"), PARTS * (t - 1) + k + 1, alone=True)
                act.activation(w2_part["hi"][:, k, :], w2_piece(e, k), ACT.Copy).then_inc(sem("w2_upper"), 1)

        def body(tile):
            t = tile.t
            if a_tile(t - 1):
                relu(t - 1)
            if a_tile(t + 1):
                upper_w1(t + 1)
                take_in(t + 1)
            if a_tile(t):
                upper_w2(t)

        act.wait_ge(sem("w_in"), 16 * 2 * B)
        act.wait_ge(sem("tables_ready"), 1)
        tile_loop(act, body)

    @block.tensor
    def _(pe):
        pe.wait_ge(consts_in, consts_need)
        cond_tensor(nc, pe, cond, ident, ps_h0, ps_h1, sem)
        pe.wait_ge(sem("router_in"), 16)

        def step(i, par, rows, cols, routed):
            b = 2 * i + par
            if routed:
                pe.wait_ge(sem("picked_ready"), b - 1)
                pe.matmul(ps_rank[:, 0:J * E], below, picked[:].rearrange("p j e -> p (j e)"), start=True, stop=True)
                pe.matmul(ps_rank[:, J * E:2 * J * E], ones, picked[:].rearrange("p j e -> p (j e)"),
                          start=True, stop=True).then_inc(sem("rank_done"), 1)
            if rows:
                pe.wait_ge(sem("xn_ready"), J * (b + 1))
                if not (isinstance(b, int) and b == 0):
                    pe.wait_ge(sem("hT_ready"), C * b)
                for c in range(C):
                    for j in range(J):
                        last = pe.transpose(ps_t[:, c * T + j * P:c * T + (j + 1) * P], xin_n[:, j, c * P:(c + 1) * P], ident)
                last.then_inc(sem("xnT_done"), 1)
            if cols:
                pe.wait_ge(sem("h2T_ready"), b)
                if not (isinstance(b, int) and b == 1):
                    pe.wait_ge(sem("logits_taken"), b - 1)
                for j in range(J):
                    for c in range(C):
                        last = pe.matmul(ps_logit[:, j * E:(j + 1) * E], h2T[:, c, j * P:(j + 1) * P], router[:, c, :],
                                         start=(c == 0), stop=(c == C - 1))
                last.then_inc(sem("logits_done"), 1)
                if not (isinstance(b, int) and b == 1):
                    pe.wait_ge(sem("h2_ready"), b - 1)
                for j in range(J):
                    for c in range(C):
                        last = pe.transpose(ps_back[:, j * D + c * P:j * D + (c + 1) * P], h2T[:, c, j * P:(j + 1) * P], ident)
                last.then_inc(sem("back_done"), 1)

        xin_n = keep["xn"]
        pipeline(pe, step)

        def turn_in(tile):
            t = tile.t
            pe.wait_ge(sem(f"tile_in{tile.par}"), 16 * (tile.before + 1))
            if isinstance(t, int) and t == 0:
                pe.wait_ge(sem("h2_ready"), B)
                pe.wait_ge(sem("hT_ready"), C * B)
            else:
                pe.wait_ge(sem("htokT_split"), t)
            for c in range(C):
                last = pe.transpose(ps_t[:, c * P:(c + 1) * P], htok[tile.par][:, c * P:(c + 1) * P], ident)
            last.then_inc(sem("tile_turned"), 1)

        def up(t):
            pe.wait_ge(sem("htokT_split"), t + 1)
            for k in range(PARTS):
                i, c = k // C, k % C
                pe.wait_ge(sem("w1_split"), PARTS * t + k + 1)
                if c == 0:
                    wait_free(pe, sem("hid_ready"), 2 * t + i - 1)
                for n, (a, b) in enumerate(PASSES):
                    last = pe.matmul(ps_h[i][:, :], htokT[a][:, c, :], w1_part[b][:, k, :],
                                     start=(c == 0 and n == 0), stop=(c == C - 1 and n == 2))
                last.then_inc(sem("w1_used"), 1)

        def turn_hidden(t):
            pe.wait_ge(sem("hid_ready"), 2 * (t + 1))
            wait_free(pe, sem("hidT_split"), 2 * t)
            for f in range(F):
                last = pe.transpose(ps_th[f // 4][:, (f % 4) * P:(f % 4 + 1) * P], hid[:, f * P:(f + 1) * P], ident)
            last.then_inc(sem("hid_turned"), 1)

        def down(t):
            pe.wait_ge(sem("hidT_split"), 2 * (t + 1))
            wait_free(pe, sem("y_ready"), t)
            for k in range(PARTS):
                pe.wait_ge(sem("w2_split"), PARTS * t + k + 1)
                for f in (2 * k, 2 * k + 1):
                    for n, (a, b) in enumerate(PASSES):
                        last = pe.matmul(ps_y[:, 0:D], hidT[a][:, f * P:(f + 1) * P], w2_part[b][:, k, (f % 2) * D:(f % 2 + 1) * D],
                                         start=(f == 0 and n == 0), stop=(f == F - 1 and n == 2))
                last.then_inc(sem("w2_used"), 1)

        def body(tile):
            t = tile.t
            if a_tile(t - 1):
                turn_hidden(t - 1)
            if a_tile(t):
                up(t)
            if a_tile(t + 1):
                turn_in(tile.ahead(1))
            if a_tile(t - 1):
                down(t - 1)

        tile_loop(pe, body)

    @block.vector
    def _(dve):
        xn = keep["xn"]
        dve.wait_ge(consts_in, consts_need)
        cond_vector(nc, dve, cond, vec, ps_h0, ps_h1, gamma, beta, keep, sem)
        dve.tensor_copy(count[:], region_row).then_inc(sem("count_ready"), 1)
        dve.wait_ge(sem("count_ready"), 1)

        def row_moments(b, i, par):
            dve.wait_ge(sem(f"x_in{par}"), 16 * (i + 1))
            for j in range(J):
                last = dve.bn_stats(row_stats[:, j, :], xin[par][:, j, :])
            last.then_inc(sem("row_stats_done"), 1)
            wait_free(dve, sem("row_rstd_ready"), b, alone=True)
            wait_alone(dve, sem("row_stats_done"), b + 1)
            for j in range(J):
                last = dve.bn_aggr(row_mv[:, j, :], row_stats[:, j, :])
            last.then_inc(sem("row_mv_done"), 1)
            dve.wait_ge(sem("row_mv_done"), b + 1)
            dve.tensor_scalar(row_mv[:, :, 1], row_mv[:, :, 1], 1e-5, None, ALU.add).then_inc(sem("row_var_ready"), 1)

        def normalise_rows(b, par):
            dve.wait_ge(sem("row_rstd_ready"), b + 1)
            if not (isinstance(b, int) and b == 0):
                dve.wait_ge(sem("xnT_done"), b)
            for j in range(J):
                dve.tensor_scalar(xn[:, j, :], xin[par][:, j, :], row_mv[:, j, 0:1], row_rstd[:, j:j + 1],
                                  ALU.subtract, ALU.mult).then_inc(sem("xn_ready"), 1)

        def column_moments(b):
            dve.wait_ge(sem("hT_ready"), C * (b + 1))
            for c in range(C):
                last = dve.bn_stats(col_stats[:, c, :], hT[:, c, :])
            last.then_inc(sem("col_stats_done"), 1)
            wait_alone(dve, sem("col_stats_done"), b + 1)
            for c in range(C):
                last = dve.bn_aggr(col_mv[:, c, :], col_stats[:, c, :])
            last.then_inc(sem("col_mv_done"), 1)
            dve.wait_ge(sem("col_mv_done"), b + 1)
            dve.tensor_scalar(col_mv[:, :, 1], col_mv[:, :, 1], 1e-8, None, ALU.add).then_inc(sem("col_var_ready"), 1)

        def modulate_columns(b):
            dve.wait_ge(sem("col_rstd_ready"), b + 1)
            s = Steps(dve, sem("col_step"), 3 * b)
            s.then(dve.tensor_tensor(col_scale[:], col_rstd[:], gamma[:, :, bass.ds(b, 1)].rearrange("p c b -> p (c b)"), ALU.mult))
            s.then(dve.tensor_tensor(col_mean_s[:], col_mv[:, :, 0], col_scale[:], ALU.mult))
            s.then(dve.tensor_tensor(col_shift[:], beta[:, :, bass.ds(b, 1)].rearrange("p c b -> p (c b)"), col_mean_s[:], ALU.subtract))
            if not (isinstance(b, int) and b == 0):
                dve.wait_ge(sem("back_done"), b)
            for c in range(C):
                last = dve.tensor_scalar(h2T[:, c, :], hT[:, c, :], col_scale[:, c:c + 1], col_shift[:, c:c + 1], ALU.mult, ALU.add)
            last.then_inc(sem("h2T_ready"), 1)

        ROUTE_STEPS = 16

        def route(b, own, par):
            s = Steps(dve, sem("route_step"), ROUTE_STEPS * b)
            dve.wait_ge(sem("logits_done"), b + 1)
            dve.tensor_copy(logits[:], ps_logit[:, 0:J * E].rearrange("p (j e) -> p j e", j=J)).then_inc(sem("logits_taken"), 1)
            wait_alone(dve, sem("logits_taken"), b + 1)
            for j in range(J):
                last = dve.max(best[:, j, :], logits[:, j, :])
            s.then_alone(last)
            for j in range(J):
                last = dve.max_index(best_at[:, j, :], best[:, j, :], logits[:, j, :])
            s.did(last)
            dve.tensor_tensor(gap[:], best[:, :, 1], best[:, :, 0], ALU.subtract).then_inc(sem("gap_ready"), 1)
            dve.wait_ge(sem("route_step"), s.at)
            s.then(dve.tensor_copy(chosen[:], best_at[:, :, 0:K].rearrange("p j k -> p k j")))
            choice = chosen[:].rearrange("p k j -> p (k j)")
            s.then(dve.tensor_tensor(onehot[:], spread(choice, [P, K * J, E], 2), spread(slot8, [P, K * J, E], 1), ALU.is_equal))
            dve.tensor_tensor(picked[:], onehot[:, 0:J, :], onehot[:, J:2 * J, :], ALU.add).then_inc(sem("picked_ready"), 1)
            s.did(dve.tensor_copy(chosen_all[:, bass.ds(b, 1), :].rearrange("p b q -> p (b q)"), choice))
            dve.wait_ge(sem("gap_exp_ready"), b + 1)
            s.then(dve.tensor_scalar(gap_sum[:], gap_exp[:], 1.0, None, ALU.add))
            first = gates[:, bass.ds(b, 1), 0, :].rearrange("p b j -> p (b j)")
            second = gates[:, bass.ds(b, 1), 1, :].rearrange("p b j -> p (b j)")
            s.then(dve.reciprocal(gap_sum[:], gap_sum[:]))
            s.did(dve.tensor_tensor(second, gap_exp[:], gap_sum[:], ALU.mult))
            s.did(dve.tensor_copy(first, gap_sum[:]))
            dve.wait_ge(sem("rank_done"), b + 1)
            n = J * E
            s.did(dve.tensor_tensor(rank_base[:, 0, :], ps_rank[:, 0:E], count[:], ALU.add))
            s.then(dve.tensor_tensor(count_mid[:], ps_rank[:, n:n + E], count[:], ALU.add))
            s.did(dve.tensor_tensor(rank_base[:, 1, :], ps_rank[:, E:2 * E], count_mid[:], ALU.add))
            s.then(dve.tensor_tensor(count[:], ps_rank[:, n + E:n + 2 * E], count_mid[:], ALU.add))
            s.then(dve.tensor_tensor(rank_sel[:].rearrange("p (k j) e -> p k j e", k=K), onehot[:].rearrange("p (k j) e -> p k j e", k=K),
                                     spread(rank_base[:], [P, K, J, E], 1), ALU.mult))
            s.then(dve.tensor_reduce(row_f[:], rank_sel[:], X, ALU.add))
            s.did(dve.tensor_copy(row_all[:, bass.ds(b, 1), :].rearrange("p b q -> p (b q)"), row_f[:]))
            if not (isinstance(own, int) and own == 0):
                dve.wait_ge(sem(f"row_sent{par}"), 16 * K * J * own)
            dve.tensor_copy(row_i[par][:], row_f[:]).then_inc(sem("row_i_ready"), 1)

        def step(i, par, rows, cols, routed):
            b = 2 * i + par
            if rows:
                row_moments(b, i, par)
            if cols:
                column_moments(b - 1)
            if routed:
                route(b - 2, i - 1, par)
            if rows:
                normalise_rows(b, par)
            if cols:
                modulate_columns(b - 1)

        pipeline(dve, step)

        s = Steps(dve, sem("table_step"))
        s.did(dve.tensor_scalar(pad_f[:], count[:], vec[:, PART:PART + 1], None, ALU.add))
        s.then(dve.tensor_tensor(tiles_n[:], count[:], region_row, ALU.subtract))
        dve.tensor_copy(pad_i[:], pad_f[:]).then_inc(sem("pad_ready"), 1)
        s.then(dve.tensor_scalar(tiles_n[:], tiles_n[:], float(P - 1), 1.0 / P, ALU.add, ALU.mult))
        s.then(dve.tensor_scalar(tiles_n[:], tiles_n[:], -(P - 1) / (2.0 * P), MAGIC, ALU.add, ALU.add))
        s.then(dve.tensor_scalar(tiles_n[:], tiles_n[:], -MAGIC, None, ALU.add))
        s.then(dve.tensor_copy(tiles_cum[0][:], tiles_n[:]))
        now = 0
        for shift in (1, 2, 4):
            s.did(dve.tensor_copy(tiles_cum[1 - now][:, 0:shift], tiles_cum[now][:, 0:shift]))
            s.then(dve.tensor_tensor(tiles_cum[1 - now][:, shift:E], tiles_cum[now][:, shift:E], tiles_cum[now][:, 0:E - shift], ALU.add))
            now = 1 - now
        cum = tiles_cum[now]
        s.then(dve.tensor_tensor(delta[:], cum[:], tiles_n[:], ALU.subtract))
        s.then(dve.tensor_scalar(delta[:], delta[:], float(P), None, ALU.mult))
        s.then(dve.tensor_tensor(delta[:], delta[:], region_row, ALU.subtract))
        tile_no = const[0:1, TILE_NO:TILE_NO + TILES]
        s.then(dve.tensor_tensor(tiles, spread(tile_no, [1, TILES, E], 2), spread(cum[0:1, :], [1, TILES, E], 1), ALU.is_ge))
        s.then(dve.tensor_reduce(tile_e[:], tiles, X, ALU.add))
        s.then(dve.tensor_scalar(tile_e[:], tile_e[:], float(E - 1), None, ALU.min))
        s.then(dve.tensor_tensor(tiles, spread(tile_e[:], [1, TILES, E], 2), spread(slot8[0:1, :], [1, TILES, E], 1), ALU.is_equal))
        s.then(dve.tensor_tensor(tiles, tiles, spread(delta[0:1, :], [1, TILES, E], 1), ALU.mult))
        s.did(dve.tensor_reduce(tile_row[:], tiles, X, ALU.add))
        s.then(dve.tensor_scalar(tile_ok[:], tile_no, cum[0:1, E - 1:E], None, ALU.is_lt))
        s.then(dve.scalar_tensor_tensor(tile_row[:], tile_no, float(P), tile_row[:], ALU.mult, ALU.subtract))
        s.then(dve.tensor_tensor(tile_row[:], tile_row[:], tile_ok[:], ALU.mult))
        s.did(dve.tensor_copy(tile_tab[:, 0, :], tile_e[:]))
        dve.tensor_copy(tile_tab[:, 1, :], tile_row[:]).then_inc(sem("tables_ready"), 1)
        dve.wait_ge(sem("h2T_ready"), B)
        every = chosen_all[:].rearrange("p b q -> p (b q)")
        s.then(dve.tensor_tensor(big, spread(every, [P, B * K * J, E], 2), spread(slot8, [P, B * K * J, E], 1), ALU.is_equal))
        s.then(dve.tensor_tensor(big, big, spread(delta[:], [P, B * K * J, E], 1), ALU.mult))
        s.then(dve.tensor_reduce(every, big, X, ALU.add))
        s.then(dve.tensor_tensor(every, every, row_all[:].rearrange("p b q -> p (b q)"), ALU.add))
        s.did(dve.tensor_copy(out_row[:], chosen_all[:]))

        dve.wait_ge(sem("w_in"), 16 * 2 * B)
        dve.wait_ge(sem("tables_ready"), 1)

        def lower_hidden(t):
            for i in range(2):
                dve.wait_ge(sem("hidT_upper"), 2 * t + i + 1)
                cols = slice(i * 512, (i + 1) * 512)
                dve.scalar_tensor_tensor(hidT["lo"][:, cols], ps_th[i][:, :], 0.0, hidT["hi"][:, cols].bitcast(F32),
                                         ALU.max, ALU.subtract).then_inc(sem("hidT_split"), 1)

        def take_hidden(tile, i):
            t = tile.t
            dve.wait_ge(sem("w1_used"), PARTS * t + C * (i + 1))
            if i == 0:
                dve.wait_ge(sem(f"b1_in{tile.par}"), 16 * (tile.before + 1))
                wait_free(dve, sem("hid_turned"), t)
            dve.tensor_tensor(hid[:, i * 512:(i + 1) * 512], ps_h[i][:, :], b1[tile.par][:, i * 512:(i + 1) * 512],
                              ALU.add).then_inc(sem("hid_ready"), 1)

        def lower_w1(t, e, k):
            wait_alone(dve, sem("w1_upper"), PARTS * t + k + 1)
            dve.tensor_tensor(w1_part["lo"][:, k, :], w1_piece(e, k), w1_part["hi"][:, k, :].bitcast(F32),
                              ALU.subtract).then_inc(sem("w1_split"), 1)

        def lower_tokens(t):
            dve.wait_ge(sem("htokT_upper"), t + 1)
            dve.tensor_tensor(htokT["lo"][:], ps_t[:, 0:C * P].rearrange("p (c m) -> p c m", c=C), htokT["hi"][:].bitcast(F32),
                              ALU.subtract).then_inc(sem("htokT_split"), 1)

        def take_out(tile):
            t = tile.t
            dve.wait_ge(sem("w2_used"), PARTS * (t + 1))
            dve.wait_ge(sem(f"b2_in{tile.par}"), 16 * (tile.before + 1))
            wait_free(dve, sem("y_sent"), 16 * t)
            dve.tensor_tensor(y, ps_y[:, 0:D], b2[tile.par][:], ALU.add).then_inc(sem("y_ready"), 1)

        def body(tile):
            t = tile.t
            if a_tile(t + 1):
                e = dve.value_load(tile_tab[0:1, 0, bass.ds(t + 1, 1)], min_val=0, max_val=E - 1)
            if a_tile(t - 1):
                lower_hidden(t - 1)
            if a_tile(t):
                take_hidden(tile, 0)
            if a_tile(t + 1):
                lower_w1(t + 1, e, 0)
                lower_w1(t + 1, e, 1)
            if a_tile(t):
                take_hidden(tile, 1)
            if a_tile(t + 1):
                lower_tokens(t + 1)
                lower_w1(t + 1, e, 2)
                lower_w1(t + 1, e, 3)
            if a_tile(t - 1):
                take_out(tile.ahead(-1))

        tile_loop(dve, body)


PASSES = (("hi", "hi"), ("hi", "lo"), ("lo", "hi"))
PARTS = 4
UNROLL = 4


class Tile:

    def __init__(self, round_, offset):
        self.round, self.offset = round_, offset
        self.t = UNROLL * round_ + offset
        self.par = offset % 2
        self.before = UNROLL // 2 * round_ + offset // 2

    def ahead(self, n):
        return Tile(self.round, self.offset + n)


def a_tile(t):
    return not isinstance(t, int) or 0 <= t < TILES


def tile_loop(eng, body):
    rounds = (TILES - 3) // UNROLL - 1
    for t in range(-1, 2):
        body(Tile(0, t))
    with eng.Fori(0, rounds) as i:
        for u in range(2, 2 + UNROLL):
            body(Tile(i, u))
    for t in range(2 + rounds * UNROLL, TILES + 1):
        body(Tile(0, t))


def pipeline(eng, step):
    step(0, 0, True, False, False)
    step(0, 1, True, True, False)
    step(1, 0, True, True, True)
    step(1, 1, True, True, True)
    with eng.Fori(2, B // 2) as i:
        step(i, 0, True, True, True)
        step(i, 1, True, True, True)
    step(B // 2, 0, False, True, True)
    step(B // 2, 1, False, False, True)


def cond_weights(nc, sb, ada_w, sty_w2):
    return {
        "ids": sb("ids", [B, 1], U32), "emb": sb("emb", [B, SE]), "embT": sb("embT", [SE, B]),
        "hyp_w1": sb("hyp_w1", [SE, SH]), "hyp_w2": sb("hyp_w2", [SH, SH]),
        "sty_w1": sb("sty_w1", [SH, SH // 2]), "sty_w2": sty_w2,
        "ada_w": ada_w,
        "a1": sb("a1", [SH, B]), "a2": sb("a2", [SH, B]), "a3": sb("a3", [SH // 2, B]),
        "pre": sb("pre", [P, C, B]), "neg": sb("neg", [P, C, B]), "low": sb("low", [P, C, B]),
        "exp": sb("exp", [P, C, B]), "log": sb("log", [P, C, B]),
        "t_int": sb("t_int", [P, B], I32), "t": sb("t", [P, B]), "q": sb("q", [P, B]), "qh": sb("qh", [P, B]),
        "ql": sb("ql", [P, B]), "r": sb("r", [P, B]), "angle": sb("angle", [P, 2, B]), "turns": sb("turns", [P, 2, B]),
        "wave": sb("wave", [P, 2, B]), "half": sb("half", [P, 2, B]),
    }


def cond_tensor(nc, pe, w, ident, ps_a, ps_b, sem):
    pe.wait_ge(sem("emb_in"), 16)
    pe.wait_ge(sem("cond_in"), 16 * 6)
    pe.transpose(ps_a[0:SE, 0:B], w["emb"][:, :], ident[0:B, 0:B]).then_inc(sem("cond_product"), 1)
    pe.wait_ge(sem("cond_layer"), 1)
    pe.matmul(ps_b[0:SH, 0:B], w["hyp_w1"][:, :], w["embT"][:, :], start=True, stop=True).then_inc(sem("cond_product"), 1)
    pe.wait_ge(sem("cond_layer"), 2)
    pe.matmul(ps_a[0:SH, 0:B], w["hyp_w2"][:, :], w["a1"][:, :], start=True, stop=True).then_inc(sem("cond_product"), 1)
    pe.wait_ge(sem("cond_layer"), 3)
    pe.matmul(ps_b[0:SH // 2, 0:B], w["sty_w1"][:, :], w["a2"][:, :], start=True, stop=True).then_inc(sem("cond_product"), 1)
    pe.wait_ge(sem("cond_layer"), 4)
    for m in range(2 * C):
        last = pe.matmul(ps_a[:, m * B:(m + 1) * B], w["sty_w2"][:, m * P:(m + 1) * P], w["a3"][:, :], start=True, stop=True)
    last.then_inc(sem("cond_product"), 1)
    pe.wait_ge(sem("wave_ready"), 1)
    for m in range(2 * C):
        for c in range(C):
            last = pe.matmul(ps_b[:, m * B:(m + 1) * B], w["ada_w"][:, c, m * P:(m + 1) * P], w["wave"][:, c, :],
                             start=(c == 0), stop=(c == C - 1))
    last.then_inc(sem("cond_product"), 1)


def cond_scalar(nc, act, w, vec, sem):
    act.wait_ge(sem("angle_ready"), 1)
    act.activation(w["turns"][:], w["angle"][:], ACT.Sin).then_inc(sem("sine_ready"), 1)
    act.wait_ge(sem("low_ready"), 1)
    act.activation(w["exp"][:], w["low"][:], ACT.Exp).then_inc(sem("soft_exp_ready"), 1)
    act.wait_ge(sem("soft_exp_ready"), 1)
    act.activation(w["log"][:], w["exp"][:], ACT.Ln, bias=1.0).then_inc(sem("soft_log_ready"), 1)
    act.wait_ge(sem("sine_ready"), 1)
    act.activation(w["half"][:], w["turns"][:], ACT.Tanh, scale=0.5).then_inc(sem("tanh_ready"), 1)


def cond_vector(nc, dve, w, vec, ps_a, ps_b, gamma, beta, keep, sem):
    s = Steps(dve, sem("cond_step"))
    dve.wait_ge(sem("cond_in"), 16 * 6)
    s.then(dve.tensor_copy(w["t"][:], w["t_int"][:]))
    s.then(dve.tensor_scalar(w["q"][:], w["t"][:], 0.01, None, ALU.mult))
    s.then(dve.tensor_scalar(w["qh"][:], w["q"][:], 4097.0, None, ALU.mult))
    s.then(dve.tensor_tensor(w["r"][:], w["qh"][:], w["q"][:], ALU.subtract))
    s.then(dve.tensor_tensor(w["qh"][:], w["qh"][:], w["r"][:], ALU.subtract))
    s.then(dve.tensor_tensor(w["ql"][:], w["q"][:], w["qh"][:], ALU.subtract))
    s.then(dve.scalar_tensor_tensor(w["r"][:], w["qh"][:], -100.0, w["t"][:], ALU.mult, ALU.add))
    s.then(dve.scalar_tensor_tensor(w["r"][:], w["ql"][:], -100.0, w["r"][:], ALU.mult, ALU.add))
    s.then(dve.scalar_tensor_tensor(w["q"][:], w["r"][:], 0.01, w["q"][:], ALU.mult, ALU.add))
    s.then(dve.tensor_scalar(w["q"][:], w["q"][:], 4000.0, None, ALU.mult))
    for i in range(2):
        last = dve.tensor_scalar(w["angle"][:, i, :], w["q"][:], vec[:, FREQ:FREQ + 1], None, ALU.mult)
    s.then(last)
    for i in range(2):
        last = dve.tensor_scalar(w["turns"][:, i, :], w["angle"][:, i, :], 1.0 / (2 * np.pi), 0.25 * i, ALU.mult, ALU.add)
    s.then(last)
    s.then(dve.tensor_scalar(w["turns"][:], w["turns"][:], 1.5 * MAGIC, -1.5 * MAGIC, ALU.add, ALU.add))
    two_pi = [6.28125, 0.0019350051879882812, 3.0199159819e-07]
    for part in two_pi:
        s.then(dve.scalar_tensor_tensor(w["angle"][:], w["turns"][:], -part, w["angle"][:], ALU.mult, ALU.add))
    s.then(dve.tensor_scalar(w["angle"][:, 1, :], w["angle"][:, 1, :], float(np.pi / 2), None, ALU.add))
    dve.tensor_scalar(w["angle"][:], w["angle"][:], 3.1415925, -3.1415925, ALU.min, ALU.max).then_inc(sem("angle_ready"), 1)
    dve.wait_ge(sem("cond_product"), 1)
    dve.tensor_copy(w["embT"][:], ps_a[0:SE, 0:B]).then_inc(sem("cond_layer"), 1)
    dve.wait_ge(sem("cond_product"), 2)
    dve.tensor_scalar(w["a1"][:], ps_b[0:SH, 0:B], vec[:, HYP_B1:HYP_B1 + 1], 0.0, ALU.add, ALU.max).then_inc(sem("cond_layer"), 1)
    dve.wait_ge(sem("cond_product"), 3)
    dve.tensor_scalar(w["a2"][:], ps_a[0:SH, 0:B], vec[:, HYP_B2:HYP_B2 + 1], None, ALU.add).then_inc(sem("cond_layer"), 1)
    dve.wait_ge(sem("cond_product"), 4)
    dve.tensor_scalar(w["a3"][:], ps_b[0:SH // 2, 0:B], vec[0:SH // 2, STY_B1:STY_B1 + 1], 0.0, ALU.add, ALU.max).then_inc(sem("cond_layer"), 1)
    dve.wait_ge(sem("cond_product"), 5)
    for c in range(C):
        dve.tensor_scalar(w["pre"][:, c, :], ps_a[:, c * B:(c + 1) * B], vec[:, STY_B2 + c:STY_B2 + c + 1], None, ALU.add)
        last = dve.tensor_scalar(beta[:, c, :], ps_a[:, (C + c) * B:(C + c + 1) * B], vec[:, STY_B2 + C + c:STY_B2 + C + c + 1], None, ALU.add)
    s.then(last)
    s.then(dve.tensor_scalar(w["neg"][:], w["pre"][:], -1.0, None, ALU.mult))
    dve.tensor_tensor(w["low"][:], w["pre"][:], w["neg"][:], ALU.min).then_inc(sem("low_ready"), 1)
    dve.wait_ge(sem("soft_log_ready"), 1)
    s.then(dve.scalar_tensor_tensor(gamma[:], w["pre"][:], 0.0, w["log"][:], ALU.max, ALU.add))
    s.then(dve.tensor_scalar(gamma[:], gamma[:], 1e-8, None, ALU.add))
    dve.wait_ge(sem("tanh_ready"), 1)
    s.then(dve.tensor_scalar(w["half"][:], w["half"][:], 1.0, 0.5, ALU.add, ALU.mult))
    dve.tensor_tensor(w["wave"][:], w["half"][:], w["turns"][:], ALU.mult).then_inc(sem("wave_ready"), 1)
    dve.wait_ge(sem("cond_product"), 6)
    for c in range(C):
        dve.tensor_scalar(keep["scale"][:, c, :], ps_b[:, c * B:(c + 1) * B], vec[:, ADA_B + c:ADA_B + c + 1], 1.0, ALU.add, ALU.add)
        last = dve.tensor_scalar(keep["shift"][:, c, :], ps_b[:, (C + c) * B:(C + c + 1) * B],
                                 vec[:, ADA_B + C + c:ADA_B + C + c + 1], None, ALU.add)
    s.then(last)


CHUNK = 2
PIECES = H // CHUNK
RING = PIECES // 2
def by_scalar(h):
    return h % 4 != 3


def transformer(nc, ctx, io, keep):
    sems = {}

    def sem(name):
        if name not in sems:
            sems[name] = ctx.enter_context(nc.semaphore(name))
        return sems[name]

    def sb(name, shape, dt=F32):
        return ctx.enter_context(nc.sbuf_tensor(name, shape, dt))

    def bank(name):
        return ctx.enter_context(nc.psum_tensor(name, [P, 512], F32))

    const, vec, gates, out_row = keep["const"], keep["vec"], keep["gates"], keep["out_row"]
    scale, shift, xn = keep["scale"], keep["shift"], keep["xn"]
    ident = const[:, IDENT:IDENT + P]
    x_rows = io["x"].rearrange("(b j p) d -> b p j d", j=J, p=P)
    out_rows = io["out"].rearrange("(b j p) d -> b p j d", j=J, p=P)
    bias_rows = io["bias"].rearrange("b h (j p) k -> b p h j k", p=P)
    mask_rows = io["mask"].rearrange("b (j p) k -> b p j k", p=P)

    wq, wk, wv, wo = [sb(n, [P, C, D]) for n in ("wq", "wk", "wv", "wo")]
    w1 = {n: sb(f"ff1_{n}", [P, C, FF], F32R) for n in ("hi", "lo")}
    w2 = {n: sb(f"ff2_{n}", [P, F, D], F32R) for n in ("hi", "lo")}
    bv, bo, b2 = [sb(n, [P, D]) for n in ("bv", "bo", "b2")]
    q_b = sb("q_b", [P, C])
    tanh_b = sb("tanh_b", [P, F])
    minus_half = sb("minus_half2", [P, J])
    row_now = sb("row_now", [P, K * J], U32)
    gate_now = sb("gate_now", [P, K * J])
    mod_now = sb("mod_now", [P, 2, C])
    x = sb("x", [P, J, D])
    picked_rows = sb("picked_rows", [P, K * J, D])
    src = sb("src", [P, J, D])
    stats, mv, rstd = sb("stats", [P, J, 6]), sb("mv", [P, J, 2]), sb("rstd", [P, J])
    xmT = [sb(f"xmT{i}", [P, C, T]) for i in range(2)]
    part = {n: sb(n, [P, C, T], F32R) for n in ("q_hi", "q_lo", "k_hi", "k_lo")}
    q_stack = [sb(f"q_stack{i}", [P, H // 2, T]) for i in range(2)]
    k_stack = [sb(f"k_stack{i}", [P, H // 2, T]) for i in range(2)]
    V_WIDE = (P // HD) * (P + HD)
    v_pad = [sb(f"v_pad{i}", [P, J, C, V_WIDE]) for i in range(2)]
    mask = sb("mask", [P, J, T // 4], U32)
    mask_f = sb("mask_f", [P, J, T])
    bias = sb("bias", [P, RING, CHUNK, J * T])
    neg = [sb(f"neg{i}", [P, J, T]) for i in range(2)]
    neg_max = [sb(f"neg_max{i}", [P, H, J]) for i in range(2)]
    total = [sb(f"total{i}", [P, H, J]) for i in range(2)]
    prob = [sb(f"prob{i}", [P, J, T]) for i in range(2)]
    probT = [sb(f"probT{i}", [P, J, T]) for i in range(2)]
    undefined = sb("undefined", [P, H, J])
    inv = sb("inv", [P, J, H])
    invT = sb("invT", [H, T])
    ctx_raw = sb("ctx_raw", [P, C, T])
    ctxT = sb("ctxT", [P, C, T])
    x3 = sb("x3", [P, J, D])
    x3b = sb("x3b", [P, J, D])
    stats2, mv2, rstd2 = sb("stats2", [P, J, 6]), sb("mv2", [P, J, 2]), sb("rstd2", [P, J])
    h_rows = sb("h_rows", [P, J, D])
    hT = h_rows[:]
    hT_part = {n: sb(f"hT_{n}", [P, C, T], F32R) for n in ("hi", "lo")}
    tanh_f = sb("tanh_f", [P, 4, T])
    up_f = sb("up_f", [P, 4, T])
    act_part = {n: sb(f"act_{n}", [P, F, T], F32R) for n in ("hi", "lo")}
    result = x3b

    ps_s = [bank(f"ps_s{i}") for i in range(2)]
    ps_p = [bank(f"ps_p{i}") for i in range(2)]
    ps_ctx = [bank(f"ps_ctx{i}") for i in range(2)]
    ps_g = [bank(f"ps_g{i}") for i in range(2)]

    w1_raw = [buf[:].rearrange("p f t -> p (f t)") for buf in (up_f, tanh_f)]
    w2_raw = [buf[:].rearrange("p j d -> p (j d)") for buf in (ctx_raw, x3, x3b, h_rows)]

    def halves(ap):
        return ap.rearrange("p (i n) -> p i n", i=2)

    block = ctx.enter_context(nc.Block())

    @block.sync
    def _(sp):
        def load_x(n):
            wait_free(sp, sem("src_read"), n, alone=True)
            sp.dma_start(x[:], x_rows[bass.ds(n, 1)].rearrange("b p j d -> p (b j) d")).then_inc(sem("x2_in"), 16)

        def load_mask(n):
            wait_free(sp, sem("mask_taken"), n, alone=True)
            sp.dma_start(mask[:], mask_rows[bass.ds(n, 1)].rearrange("b p j k -> p (b j) k")).then_inc(sem("mask_in"), 16)

        def load_bias(n, c):
            wait_free(sp, sem("neg_ready"), J * (H * n + CHUNK * (c - RING + 1)), alone=True)
            sp.dma_start(bias[:, c % RING, :, :].rearrange("p h (j k) -> p h j k", j=J),
                         bias_rows[bass.ds(n, 1), :, c * CHUNK:(c + 1) * CHUNK].rearrange("b p h j k -> p (b h) j k")
                         ).then_inc(sem(f"bias_in{c % RING}"), 16)

        def send_parts(n):
            wait_free(sp, sem("stack_in"), 16 * 16 * n, alone=True)
            for which in ("q", "k"):
                sp.wait_ge(sem(f"{which}_split"), 2 * C * (n + 1))
                for piece in ("hi", "lo"):
                    name = f"{which}_{piece}"
                    sp.dma_start(io[name].rearrange("(m p) t -> p m t", p=P), part[name][:].bitcast(F32)).then_inc(sem("split_sent"), 16)

        def bring_stacks(n, par):
            sp.wait_ge(sem("split_sent"), 64 * (n + 1))
            if n_int_or(n) >= 2:
                sp.wait_ge(sem("scores_done"), H * (n - 1))
            for which, dst, order in (("q", q_stack[par], ("hi", "lo", "hi", "lo")), ("k", k_stack[par], ("hi", "hi", "lo", "lo"))):
                for term, piece in enumerate(order):
                    rows = io[f"{which}_{piece}"].rearrange("(s i d) t -> i d s t", i=2, d=HD)
                    for i in range(2):
                        at = i * 64 + term * HD
                        sp.dma_start(dst[at:at + HD, :, :], rows[i]).then_inc(sem("stack_in"), 16)

        def step(n, par):
            starting = isinstance(n, int) and n < 0
            if exists(n + 2):
                load_x(n + 2)
            if exists(n):
                load_bias(n, RING)
                load_bias(n, RING + 1)
            if exists(n - 2):
                sp.wait_ge(sem("result_ready"), n - 1)
                sp.dma_start(out_rows[bass.ds(n - 2, 1)].rearrange("b p j d -> p (b j) d"), result[:]).then_inc(sem("out_sent"), 16)
            if exists(n + 1):
                load_mask(n + 1)
                if starting:
                    load_bias(n + 1, 0)
            if exists(n):
                load_bias(n, RING + 2)
            if exists(n + 1):
                send_parts(n + 1)
            if exists(n):
                load_bias(n, RING + 3)
            if exists(n + 1):
                bring_stacks(n + 1, 1 - par)
            if exists(n + 1):
                for c in range(1 if starting else 0, RING):
                    load_bias(n + 1, c)

        entries(sp, step)
        sp.wait_ge(sem("out_sent"), 16 * B)

    @block.gpsimd
    def _(pool):
        pool.memset(minus_half[:], -0.5).then_inc(sem("half_set2"), 1)
        pool.wait_ge(sem("half_set2"), 1)

        def rsqrt(out, var, ready, done, n):
            pool.wait_ge(sem(ready), n + 1)
            pool.tensor_tensor(out[:], var[:, :, 1], minus_half[:], ALU.pow).then_inc(sem(done), 1)

        def gather(n):
            wait_free(pool, sem("src_read"), n)
            wait_free(pool, sem("xmT_ready"), C * n)
            pool.tensor_copy(gate_now[:], gates[:, bass.ds(n, 1), :, :].rearrange("p b k j -> p (b k j)")).then_inc(sem("entry_cols"), 1)
            pool.tensor_copy(mod_now[:, 0, :], scale[:, :, bass.ds(n, 1)].rearrange("p c b -> p (c b)")).then_inc(sem("entry_cols"), 1)
            pool.tensor_copy(mod_now[:, 1, :], shift[:, :, bass.ds(n, 1)].rearrange("p c b -> p (c b)")).then_inc(sem("entry_cols"), 1)
            pool.tensor_copy(row_now[:], out_row[:, bass.ds(n, 1), :].rearrange("p b q -> p (b q)")).then_inc(sem("entry_cols"), 1)
            wait_alone(pool, sem("entry_cols"), 4 * (n + 1))
            for q in range(K * J):
                pool.indirect_dma_start(picked_rows[:, q, :], None, io["expert_out"],
                                        bass.IndirectOffsetOnAxis(ap=row_now[:, q:q + 1], axis=0),
                                        bounds_check=TILES * P - 1, oob_is_err=False).then_inc(sem("rows_in"), 16)

        def add_mask(n, c):
            wait_alone(pool, sem(f"bias_in{c % RING}"), 16 * (2 * n + c // RING + 1))
            pool.wait_ge(sem("mask_taken"), n + 1)
            pool.tensor_tensor(bias[:, c % RING, :, :], bias[:, c % RING, :, :],
                               spread(mask_f[:].rearrange("p j k -> p (j k)"), [P, CHUNK, J * T], 1), ALU.add
                               ).then_inc(sem("bias_masked"), 1)

        def lower_gelu(n, pair):
            wait_alone(pool, sem("act_upper"), 4 * n + pair + 1)
            at = 2 * pair % 4
            pool.tensor_tensor(act_part["lo"][:, 2 * pair:2 * pair + 2, :], up_f[:, at:at + 2, :],
                               act_part["hi"][:, 2 * pair:2 * pair + 2, :].bitcast(F32), ALU.subtract).then_inc(sem("act_split"), 1)

        def take_mask(n):
            wait_alone(pool, sem("mask_in"), 16 * (n + 1))
            wait_free(pool, sem("bias_masked"), PIECES * n, alone=True)
            pool.tensor_scalar(mask_f[:], mask[:].bitcast(U8), MASKED, None, ALU.mult).then_inc(sem("mask_taken"), 1)

        def step(n, par):
            starting = isinstance(n, int) and n < 0
            if exists(n):
                add_mask(n, RING - 1)
                add_mask(n, RING)
            if exists(n - 1):
                rsqrt(rstd2, mv2, "var2_ready", "rstd2_ready", n - 1)
            if exists(n):
                add_mask(n, RING + 1)
            if exists(n + 2):
                gather(n + 2)
            if exists(n):
                add_mask(n, RING + 2)
                add_mask(n, RING + 3)
            if exists(n + 1):
                take_mask(n + 1)
                if starting:
                    add_mask(n + 1, 0)
            if exists(n + 2) and starting:
                rsqrt(rstd, mv, "var_ready", "rstd_ready", n + 2)
            if exists(n - 1):
                lower_gelu(n - 1, 0)
                lower_gelu(n - 1, 1)
            if exists(n + 1) and not starting:
                add_mask(n + 1, 0)
            if exists(n - 1):
                lower_gelu(n - 1, 2)
                lower_gelu(n - 1, 3)
            if exists(n + 1):
                add_mask(n + 1, 1)
                add_mask(n + 1, 2)
            if exists(n + 2) and not starting:
                rsqrt(rstd, mv, "var_ready", "rstd_ready", n + 2)

        entries(pool, step)

    @block.scalar
    def _(act):
        for dst, name in ((wq, "wq"), (wk, "wk"), (wv, "wv")):
            act.dma_start(dst[:], io[name]).then_inc(sem("qkv_in"), 16)
        act.dma_start(bv[:], io["rows"][0].partition_broadcast(P)).then_inc(sem("qkv_in"), 16)
        act.wait_ge(sem("rows_in"), 16 * K * J)
        for i, dst in enumerate((bo, b2)):
            act.dma_start(dst[:], io["rows"][1 + i].partition_broadcast(P)).then_inc(sem("layer_in"), 16)
        act.dma_start(wo[:], io["wo"]).then_inc(sem("layer_in"), 16)
        for c, dst in enumerate(w1_raw):
            act.dma_start(dst, io["ff_w1"][:, c, :]).then_inc(sem("layer_in"), 16)
        for i, dst in enumerate(w2_raw):
            act.dma_start(dst, io["ff_w2"][:, 2 * i:2 * i + 2, :].rearrange("p f d -> p (f d)")).then_inc(sem("layer_in"), 16)

        def exponentials(n, h, par):
            act.wait_ge(sem("neg_ready"), J * (H * n + h + 1))
            wait_free(act, sem("p_turned"), H * n + h - 1)
            for j in range(J):
                act.activation(prob[h % 2][:, j, :], neg[h % 2][:, j, :], ACT.Exp, scale=-1.0,
                               bias=neg_max[par][:, h, j:j + 1], accum_out=total[par][:, h, j:j + 1]).then_inc(sem("p_ready"), 1)

        def take_probT(n, h):
            act.wait_ge(sem("p_turned"), H * n + h + 1)
            wait_free(act, sem("pv_done"), H * n + h - 1)
            act.activation(probT[h % 2][:], halves(ps_p[h % 2][:, :]), ACT.Copy).then_inc(sem("pT_scalar"), 1)

        def modulate(n, par):
            act.wait_ge(sem("xnT2_done"), n + 1)
            act.wait_ge(sem("entry_cols"), 4 * (n + 1))
            wait_free(act, sem("wo_done"), n - 1)
            for c in range(C):
                act.activation(xmT[par][:, c, :], ps_g[1][:, c * T:(c + 1) * T], ACT.Identity, bias=mod_now[:, 1, c:c + 1],
                               scale=mod_now[:, 0, c:c + 1]).then_inc(sem("xmT_ready"), 1)

        def upper(n, which, g, shift_by):
            act.wait_ge(sem(f"{which}_done"), n + 1)
            wait_free(act, sem("split_sent"), 64 * n)
            for m in range(C):
                act.activation(part[f"{which}_hi"][:, m, :], ps_g[g][:, m * T:(m + 1) * T], ACT.Identity,
                               bias=shift_by[:, m:m + 1]).then_inc(sem(f"{which}_split"), 1)

        def take_ctx(n, g):
            act.wait_ge(sem("pv_done"), H * n + (g + 1) * (H // 2))
            wait_free(act, sem("ctxT_ready"), n)
            act.activation(ctx_raw[:, g, :], ps_ctx[g][:, 0:T], ACT.Copy).then_inc(sem("ctx_taken"), 1)

        def take_hT(n):
            act.wait_ge(sem("h_turned"), n + 1)
            wait_free(act, sem("hT_split"), n)
            for c in range(C):
                act.activation(hT[:, c, :], ps_g[1][:, c * T:(c + 1) * T], ACT.Identity, bias=vec[:, LN2_B + c:LN2_B + c + 1],
                               scale=vec[:, LN2_G + c:LN2_G + c + 1]).then_inc(sem("hT2_ready"), 1)

        def tanh(n, pair):
            act.wait_ge(sem("ff1_done"), 4 * n + pair + 1)
            wait_free(act, sem("gelu_ready"), 4 * n + pair - 1)
            for i in range(2):
                f = 2 * pair + i
                act.activation(tanh_f[:, f % 4, :], ps_g[1 - pair % 2][:, i * T:(i + 1) * T], ACT.Tanh, bias=tanh_b[:, f:f + 1],
                               scale=0.851).then_inc(sem("tanh2_ready"), 1)

        def upper_gelu(n, pair):
            act.wait_ge(sem("gelu_ready"), 4 * n + pair + 1)
            wait_free(act, sem("ff2_done"), n)
            at = 2 * pair % 4
            act.activation(act_part["hi"][:, 2 * pair:2 * pair + 2, :], up_f[:, at:at + 2, :], ACT.Copy).then_inc(sem("act_upper"), 1)

        def step(n, par):
            for h in range(H):
                ahead, head = neighbour(n, h, 1)
                if exists(ahead):
                    exponentials(ahead, head, par if head else 1 - par)
                if exists(n) and by_scalar(h):
                    take_probT(n, h)
                if h == 0 and exists(n - 1):
                    take_ctx(n - 1, 1)
                if h == 8 and exists(n):
                    take_ctx(n, 0)
                if isinstance(n, int) and n == 0 and h == 8:
                    act.wait_ge(sem("setup_done"), 2)
                if exists(n + 1):
                    if h == 3:
                        modulate(n + 1, 1 - par)
                    if h == 4:
                        upper(n + 1, "q", 1, q_b)
                    if h == 5:
                        upper(n + 1, "k", 0, vec[:, K_B:K_B + C])
                if exists(n - 1):
                    if h == 6:
                        take_hT(n - 1)
                    if 9 <= h < 13:
                        upper_gelu(n - 1, h - 9)
                    if 7 <= h < 11:
                        tanh(n - 1, h - 7)

        act.wait_ge(sem("setup_done"), 1)
        entries(act, step)

    @block.tensor
    def _(pe):
        def scores(n, h, par):
            if h == 0:
                wait_alone(pe, sem("stack_in"), 256 * (n + 1))
            wait_free(pe, sem("neg_ready"), J * (H * n + h - 1), alone=True)
            rows = slice((h % 2) * 64, (h % 2) * 64 + 64)
            for j in range(J):
                last = pe.matmul(ps_s[h % 2][:, j * T:(j + 1) * T], q_stack[par][rows, h // 2, j * P:(j + 1) * P].bitcast(F32R),
                                 k_stack[par][rows, h // 2, :].bitcast(F32R), start=True, stop=True)
            last.then_inc(sem("scores_done"), 1)

        def turn_probs(n, h):
            pe.wait_ge(sem("p_ready"), J * (H * n + h + 1))
            before, head = neighbour(n, h, -2)
            if exists(before):
                wait_probT(pe, before, head)
            for kt in range(J):
                for j in range(J):
                    last = pe.transpose(ps_p[h % 2][:, kt * T + j * P:kt * T + (j + 1) * P], prob[h % 2][:, j, kt * P:(kt + 1) * P], ident)
            last.then_inc(sem("p_turned"), 1)

        def weigh(n, h, par):
            wait_probT(pe, n, h)
            g, i = h // (H // 2), h % (H // 2)
            if h == 0:
                pe.wait_ge(sem("v_ready"), J * (n + 1))
            if i == 0:
                wait_free(pe, sem("ctx_taken"), C * n + g - 1)
            for kt in range(J):
                last = pe.matmul(ps_ctx[g][:, 0:T], v_pad[par][:, kt, g, i * P:(i + 1) * P], probT[h % 2][:, kt, :],
                                 start=(i == 0 and kt == 0), stop=(i == H // 2 - 1 and kt == J - 1))
            last.then_inc(sem("pv_done"), 1)

        def wait_probT(eng, n, h):
            if by_scalar(h):
                eng.wait_ge(sem("pT_scalar"), 12 * n + h - h // 4 + 1)
            else:
                eng.wait_ge(sem("pT_vector"), 4 * n + h // 4 + 1)

        def turn_inv(n):
            pe.wait_ge(sem("inv_ready"), n + 1)
            wait_free(pe, sem("gelu_ready"), 4 * n)
            for j in range(J):
                last = pe.transpose(ps_g[1][0:H, j * P:(j + 1) * P], inv[:, j, :], ident)
            last.then_inc(sem("inv_turned"), 1)

        def spread_inv(n):
            wait_alone(pe, sem("invT_ready"), n + 1)
            wait_free(pe, sem("result_ready"), n, alone=True)
            for m in range(C):
                last = pe.matmul(ps_g[0][:, m * T:(m + 1) * T], const[0:H, SPREAD + m * P:SPREAD + (m + 1) * P], invT[:, :],
                                 start=True, stop=True)
            last.then_inc(sem("inv_spread"), 1)

        def turn_x(n):
            pe.wait_ge(sem("xn2_ready"), J * (n + 1))
            wait_free(pe, sem("invT_ready"), n - 1)
            for c in range(C):
                for j in range(J):
                    last = pe.transpose(ps_g[1][:, c * T + j * P:c * T + (j + 1) * P], xn[:, j, c * P:(c + 1) * P], ident)
            last.then_inc(sem("xnT2_done"), 1)

        def output(n, par):
            pe.wait_ge(sem("ctxT_ready"), n + 1)
            for j in range(J):
                for m in range(C):
                    sums = ps_g[0][:, j * D + m * P:j * D + (m + 1) * P]
                    for c in range(C):
                        pe.matmul(sums, ctxT[:, c, j * P:(j + 1) * P], wo[:, c, m * P:(m + 1) * P], start=(c == 0), stop=False)
                    last = pe.matmul(sums, xmT[par][:, m, j * P:(j + 1) * P], ident, start=False, stop=True)
            last.then_inc(sem("wo_done"), 1)

        def query_or_key(n, par, which, w, g):
            if which == "q":
                pe.wait_ge(sem("xmT_ready"), C * (n + 1))
            else:
                wait_free(pe, sem("x3_ready"), n - 1)
            for m in range(C):
                for c in range(C):
                    last = pe.matmul(ps_g[g][:, m * T:(m + 1) * T], w[:, c, m * P:(m + 1) * P], xmT[par][:, c, :],
                                     start=(c == 0), stop=(c == C - 1))
            last.then_inc(sem(f"{which}_done"), 1)

        def values(n, par):
            pe.wait_ge(sem("k_split"), 2 * C * (n + 1))
            for kt in range(J):
                for c in range(C):
                    last = pe.matmul(ps_g[0][:, kt * D:(kt + 1) * D], xmT[par][:, c, kt * P:(kt + 1) * P], wv[:, c, :],
                                     start=(c == 0), stop=(c == C - 1))
            last.then_inc(sem("v_done"), 1)

        def turn_h(n):
            pe.wait_ge(sem("h_rows_ready"), J * (n + 1))
            if exists(n + 2):
                pe.wait_ge(sem("q_split"), 2 * C * (n + 3))
            for c in range(C):
                for j in range(J):
                    last = pe.transpose(ps_g[1][:, c * T + j * P:c * T + (j + 1) * P], h_rows[:, j, c * P:(c + 1) * P], ident)
            last.then_inc(sem("h_turned"), 1)

        def feed_up(n, pair):
            if pair == 0:
                pe.wait_ge(sem("hT_split"), n + 1)
            elif pair == 1:
                if exists(n + 2):
                    pe.wait_ge(sem("v_ready"), J * (n + 3))
            else:
                pe.wait_ge(sem("gelu_ready"), 4 * n + pair - 1)
            for i in range(2):
                f = 2 * pair + i
                for c in range(C):
                    for k, (a, b) in enumerate(PASSES):
                        last = pe.matmul(ps_g[1 - pair % 2][:, i * T:(i + 1) * T], w1[a][:, c, f * P:(f + 1) * P], hT_part[b][:, c, :],
                                         start=(c == 0 and k == 0), stop=(c == C - 1 and k == 2))
            last.then_inc(sem("ff1_done"), 1)

        def feed_down(n, quarter):
            j, half = quarter // 2, quarter % 2
            pe.wait_ge(sem("gelu_ready"), 4 * n + 4)
            pe.wait_ge(sem("act_split"), 4 * n + (4 if quarter else 2))
            for f in range(4 * half, 4 * half + 4):
                for k, (a, b) in enumerate(PASSES):
                    last = pe.matmul(ps_g[0][:, j * D:(j + 1) * D], act_part[a][:, f, j * P:(j + 1) * P], w2[b][:, f, :],
                                     start=(f == 0 and k == 0), stop=(f == F - 1 and k == 2))
            if quarter == 3:
                last.then_inc(sem("ff2_done"), 1)

        def step(n, par):
            for h in range(H):
                ahead, head = neighbour(n, h, 2)
                if exists(ahead):
                    scores(ahead, head, par if head >= 2 else 1 - par)
                if exists(n):
                    turn_probs(n, h)
                if isinstance(n, int) and n == 1 and h == 0:
                    pe.wait_ge(sem("setup_done"), 2)
                if exists(n - 1):
                    if h == 0:
                        turn_inv(n - 1)
                    if h == 1:
                        spread_inv(n - 1)
                    if h == 3:
                        output(n - 1, 1 - par)
                if exists(n + 1):
                    if h == 2:
                        turn_x(n + 1)
                    if h == 4:
                        query_or_key(n + 1, 1 - par, "q", wq, 1)
                    if h == 5:
                        query_or_key(n + 1, 1 - par, "k", wk, 0)
                if exists(n - 1) and h == 6:
                    turn_h(n - 1)
                if exists(n + 1) and h == 6:
                    values(n + 1, 1 - par)
                if exists(n - 1):
                    if 7 <= h < 11:
                        feed_up(n - 1, h - 7)
                    if h >= 12:
                        feed_down(n - 1, h - 12)
                before, head = neighbour(n, h, -1)
                if exists(before):
                    weigh(before, head, par if head < H - 1 else 1 - par)

        pe.wait_ge(sem("setup_done"), 1)
        entries(pe, step)

    @block.vector
    def _(dve):
        def chain(name, count, n):
            return Steps(dve, sem(name), count * n)

        def combine_first(n):
            wait_free(dve, sem("xn2_ready"), J * n)
            dve.wait_ge(sem("x2_in"), 16 * (n + 1))
            dve.wait_ge(sem("rows_in"), 16 * K * J * (n + 1))
            dve.wait_ge(sem("entry_cols"), 4 * (n + 1))
            for j in range(J):
                last = dve.scalar_tensor_tensor(src[:, j, :], picked_rows[:, j, :], gate_now[:, j:j + 1], x[:, j, :], ALU.mult, ALU.add)
            last.then_inc(sem("src_started"), 1)

        def combine_second(n):
            dve.wait_ge(sem("src_started"), n + 1)
            for j in range(J):
                last = dve.scalar_tensor_tensor(src[:, j, :], picked_rows[:, J + j, :], gate_now[:, J + j:J + j + 1], src[:, j, :],
                                                ALU.mult, ALU.add)
            last.then_inc(sem("src_read"), 1)

        def input_moments(n):
            s = chain("src_step", 2, n)
            wait_alone(dve, sem("src_read"), n + 1)
            for j in range(J):
                last = dve.bn_stats(stats[:, j, :], src[:, j, :])
            s.then_alone(last)
            for j in range(J):
                last = dve.bn_aggr(mv[:, j, :], stats[:, j, :])
            s.then(last)
            dve.tensor_scalar(mv[:, :, 1], mv[:, :, 1], 1e-5, None, ALU.add).then_inc(sem("var_ready"), 1)

        def normalise(n):
            dve.wait_ge(sem("rstd_ready"), n + 1)
            for j in range(J):
                dve.tensor_scalar(xn[:, j, :], src[:, j, :], mv[:, j, 0:1], rstd[:, j:j + 1],
                                  ALU.subtract, ALU.mult).then_inc(sem("xn2_ready"), 1)

        def minimum(n, h, par):
            wait_alone(dve, sem("scores_done"), H * n + h + 1)
            if h % CHUNK == 0:
                wait_alone(dve, sem("bias_masked"), PIECES * n + h // CHUNK + 1)
            wait_free(dve, sem("p_ready"), J * (H * n + h - 1), alone=True)
            for j in range(J):
                dve.tensor_tensor_reduce(neg[h % 2][:, j, :], ps_s[h % 2][:, j * T:(j + 1) * T],
                                         bias[:, h // CHUNK % RING, h % CHUNK, j * T:(j + 1) * T], -1.0, -MASKED,
                                         ALU.add, ALU.min, neg_max[par][:, h, j:j + 1]).then_inc(sem("neg_ready"), 1)

        def take_probT(n, h):
            dve.wait_ge(sem("p_turned"), H * n + h + 1)
            wait_free(dve, sem("pv_done"), H * n + h - 1)
            dve.tensor_copy(probT[h % 2][:], halves(ps_p[h % 2][:, :])).then_inc(sem("pT_vector"), 1)

        def inverse(n, par):
            s = chain("inv_step", 2, n)
            dve.wait_ge(sem("p_ready"), J * H * (n + 1))
            wait_free(dve, sem("inv_turned"), n)
            s.did(dve.tensor_scalar(undefined[:], neg_max[par][:], 1e10, 0.0, ALU.mult, ALU.mult))
            s.then(dve.reciprocal(inv[:].rearrange("p j h -> p h j"), total[par][:]))
            dve.tensor_tensor(inv[:], inv[:], undefined[:].rearrange("p h j -> p j h"), ALU.add).then_inc(sem("inv_ready"), 1)

        def take_inv(n):
            dve.wait_ge(sem("inv_turned"), n + 1)
            wait_free(dve, sem("inv_spread"), n)
            dve.tensor_copy(invT[:], ps_g[1][0:H, 0:T]).then_inc(sem("invT_ready"), 1)

        def scale_ctx(n):
            dve.wait_ge(sem("inv_spread"), n + 1)
            dve.wait_ge(sem("ctx_taken"), C * (n + 1))
            wait_free(dve, sem("wo_done"), n)
            dve.tensor_tensor(ctxT[:], ctx_raw[:], halves(ps_g[0][:, :]), ALU.mult).then_inc(sem("ctxT_ready"), 1)

        def lower(n, which, g, shift_by):
            dve.wait_ge(sem(f"{which}_split"), C * (2 * n + 1))
            for m in range(C):
                dve.scalar_tensor_tensor(part[f"{which}_lo"][:, m, :], ps_g[g][:, m * T:(m + 1) * T], shift_by[:, m:m + 1],
                                         part[f"{which}_hi"][:, m, :].bitcast(F32), ALU.add, ALU.subtract).then_inc(sem(f"{which}_split"), 1)

        def take_values(n, par):
            dve.wait_ge(sem("v_done"), n + 1)
            if n_int_or(n) >= 2:
                dve.wait_ge(sem("pv_done"), H * (n - 1))
            for kt in range(J):
                dve.tensor_tensor(v_pad[par][:, kt, :, :].rearrange("p g (i w) -> p g i w", w=P + HD)[:, :, :, 0:HD],
                                  ps_g[0][:, kt * D:(kt + 1) * D].rearrange("p (g i w) -> p g i w", g=C, w=HD),
                                  bv[:].rearrange("p (g i w) -> p g i w", g=C, w=HD), ALU.add).then_inc(sem("v_ready"), 1)

        def residual(n):
            dve.wait_ge(sem("wo_done"), n + 1)
            wait_free(dve, sem("h_rows_ready"), J * n)
            dve.tensor_tensor(x3[:], halves(ps_g[0][:, :]), spread(bo[:], [P, J, D], 1), ALU.add).then_inc(sem("x3_ready"), 1)

        def moments(n):
            s = chain("ln2_step", 2, n)
            wait_alone(dve, sem("x3_ready"), n + 1)
            for j in range(J):
                last = dve.bn_stats(stats2[:, j, :], x3[:, j, :])
            s.then_alone(last)
            wait_free(dve, sem("rstd2_ready"), n, alone=True)
            for j in range(J):
                last = dve.bn_aggr(mv2[:, j, :], stats2[:, j, :])
            s.then(last)
            dve.tensor_scalar(mv2[:, :, 1], mv2[:, :, 1], 1e-5, None, ALU.add).then_inc(sem("var2_ready"), 1)

        def prepare_sum(n):
            wait_free(dve, sem("out_sent"), 16 * n)
            dve.tensor_tensor(x3b[:], x3[:], spread(b2[:], [P, J, D], 1), ALU.add).then_inc(sem("x3b_ready"), 1)

        def normalise2(n):
            dve.wait_ge(sem("rstd2_ready"), n + 1)
            wait_free(dve, sem("hT_split"), n)
            for j in range(J):
                dve.tensor_scalar(h_rows[:, j, :], x3[:, j, :], mv2[:, j, 0:1], rstd2[:, j:j + 1],
                                  ALU.subtract, ALU.mult).then_inc(sem("h_rows_ready"), 1)

        def split_hT(n):
            dve.wait_ge(sem("hT2_ready"), C * (n + 1))
            wait_free(dve, sem("ff1_done"), 4 * n)
            dve.tensor_copy(hT_part["hi"][:], hT).then_inc(sem("hT_upper"), 1)
            dve.wait_ge(sem("hT_upper"), n + 1)
            dve.tensor_tensor(hT_part["lo"][:], hT, hT_part["hi"][:].bitcast(F32), ALU.subtract).then_inc(sem("hT_split"), 1)

        def gelu(n, pair):
            dve.wait_ge(sem("tanh2_ready"), F * n + 2 * pair + 2)
            wait_free(dve, sem("act_split"), 4 * n + pair - 1)
            for i in range(2):
                f = 2 * pair + i
                dve.tensor_scalar(up_f[:, f % 4, :], ps_g[1 - pair % 2][:, i * T:(i + 1) * T], vec[:, FF_B1 + f:FF_B1 + f + 1], None,
                                  ALU.add).then_inc(sem("up_ready"), 1)
            dve.wait_ge(sem("up_ready"), F * n + 2 * pair + 2)
            at = 2 * pair % 4
            dve.scalar_tensor_tensor(up_f[:, at:at + 2, :], tanh_f[:, at:at + 2, :], 1.0, up_f[:, at:at + 2, :],
                                     ALU.add, ALU.mult).then_inc(sem("gelu_ready"), 1)

        def finish(n):
            dve.wait_ge(sem("ff2_done"), n + 1)
            dve.wait_ge(sem("x3b_ready"), n + 1)
            dve.tensor_tensor(result[:], halves(ps_g[0][:, :]), x3b[:], ALU.add).then_inc(sem("result_ready"), 1)

        def prepare_attention():
            dve.wait_ge(sem("qkv_in"), 16 * 4)
            dve.tensor_scalar(wq[:], wq[:], 1.0 / 4, None, ALU.mult)
            dve.tensor_scalar(q_b[:], vec[:, Q_B:Q_B + C], 1.0 / 4, None, ALU.mult)
            dve.tensor_scalar(tanh_b[:], vec[:, FF_B1:FF_B1 + F], 0.851, None, ALU.mult).then_inc(sem("setup_done"), 1)

        def prepare_rest():
            dve.wait_ge(sem("layer_in"), 16 * 9)
            for c in range(C):
                dve.tensor_copy(w1["hi"][:, c, :], w1_raw[c]).then_inc(sem("w_upper"), 1)
            for i in range(4):
                dve.tensor_scalar(w2["hi"][:, 2 * i:2 * i + 2, :].rearrange("p f d -> p (f d)"), w2_raw[i], 0.5, None,
                                  ALU.mult).then_inc(sem("w_upper"), 1)
            dve.wait_ge(sem("w_upper"), C + 4)
            for c in range(C):
                dve.tensor_tensor(w1["lo"][:, c, :], w1_raw[c], w1["hi"][:, c, :].bitcast(F32), ALU.subtract)
            for i in range(4):
                last = dve.scalar_tensor_tensor(w2["lo"][:, 2 * i:2 * i + 2, :].rearrange("p f d -> p (f d)"), w2_raw[i], 0.5,
                                                w2["hi"][:, 2 * i:2 * i + 2, :].rearrange("p f d -> p (f d)").bitcast(F32),
                                                ALU.mult, ALU.subtract)
            last.then_inc(sem("setup_done"), 1)

        def step(n, par):
            if isinstance(n, int) and n == -1:
                normalise(0)
                prepare_attention()
            for h in range(H):
                ahead, head = neighbour(n, h, 1)
                if exists(ahead):
                    minimum(ahead, head, par if head else 1 - par)
                if exists(n) and not by_scalar(h):
                    take_probT(n, h)
                if exists(n - 2) and h == 0:
                    finish(n - 2)
                if exists(n - 1):
                    if h == 0:
                        take_inv(n - 1)
                    if h == 1:
                        scale_ctx(n - 1)
                    if h == 4:
                        residual(n - 1)
                        moments(n - 1)
                    if h == 5:
                        normalise2(n - 1)
                    if 8 <= h < 12:
                        gelu(n - 1, h - 8)
                    if h == 7:
                        prepare_sum(n - 1)
                if exists(n + 1):
                    if h == 0 and not (isinstance(n, int) and n == -1):
                        normalise(n + 1)
                    if h == 5:
                        lower(n + 1, "q", 1, q_b)
                    if h == 6:
                        if isinstance(n, int) and n == -1:
                            dve.wait_ge(sem("v_zeroed"), 2)
                        lower(n + 1, "k", 0, vec[:, K_B:K_B + C])
                if h == 6 and exists(n - 1):
                    split_hT(n - 1)
                if h == 6 and exists(n + 1):
                    take_values(n + 1, 1 - par)
                if exists(n + 2):
                    if h == 12:
                        combine_first(n + 2)
                    if h == 13:
                        combine_second(n + 2)
                    if h == 14:
                        input_moments(n + 2)
                if h == H - 1 and exists(n):
                    inverse(n, par)
                if isinstance(n, int) and n == -1 and h == H - 1:
                    prepare_rest()
                    dve.wait_ge(sem("setup_done"), 2)

        for i in range(2):
            dve.memset(v_pad[i][:], 0.0).then_inc(sem("v_zeroed"), 1)
        entries(dve, step)


def n_int_or(n):
    return n if isinstance(n, int) else B


def layers(nc, io):
    with ExitStack() as ctx:
        keep = {
            "const": ctx.enter_context(nc.sbuf_tensor("const", [P, CONSTS], F32)),
            "vec": ctx.enter_context(nc.sbuf_tensor("vec", [P, VECS], F32)),
            "gates": ctx.enter_context(nc.sbuf_tensor("gates", [P, B, K, J], F32)),
            "out_row": ctx.enter_context(nc.sbuf_tensor("out_row", [P, B, K * J], U32)),
            "scale": ctx.enter_context(nc.sbuf_tensor("scale", [P, C, B], F32)),
            "shift": ctx.enter_context(nc.sbuf_tensor("shift", [P, C, B], F32)),
            "xn": ctx.enter_context(nc.sbuf_tensor("xn", [P, J, D], F32)),
            "consts_in": ctx.enter_context(nc.semaphore("consts_in")),
        }
        io["dispatch"] = nc.dram_tensor("dispatch", (E * REGION, D), F32, kind="Internal").ap()
        io["expert_out"] = nc.dram_tensor("expert_out", (TILES * P, D), F32, kind="Internal").ap()
        for name in ("q_hi", "q_lo", "k_hi", "k_lo"):
            io[name] = nc.dram_tensor(name + "_rows", (D, T), F32, kind="Internal").ap()
        with ExitStack() as first:
            condition_and_route(nc, first, io, keep)
        with ExitStack() as second:
            transformer(nc, second, io, keep)


def kernel(**inputs):
    import concourse.bacc as bacc
    from concourse.bass_utils import run_bass_kernel_spmd

    given = {k: np.asarray(v) for k, v in inputs.items()}

    def first(name):
        return given["L0_cond_" + name]

    def second(name):
        return given["L1_cond_" + name]

    def columns(v):
        return np.pad(v, (0, -len(v) % P)).reshape(-1, P).T

    def chunks(w):
        return np.ascontiguousarray(w.reshape(-1, P, w.shape[-1]).transpose(1, 0, 2))

    freq = np.exp(np.arange(D // 2, dtype=np.float32) * np.float32(-np.log(10000.0) / (D // 2 - 1))).astype(np.float32)
    const = np.zeros((P, CONSTS), np.float32)
    const[:, IDENT:IDENT + P] = np.eye(P)
    const[:, BELOW:BELOW + P] = np.triu(np.ones((P, P)), 1)
    const[:, ONES:ONES + P] = 1
    const[:, SLOT:SLOT + E] = np.arange(E)
    const[:, TILE_NO:TILE_NO + TILES] = np.arange(TILES)
    const[:, REGION_ROW:REGION_ROW + E] = np.arange(E) * REGION
    const[0:H, SPREAD:SPREAD + D] = np.kron(np.eye(H), np.ones((1, HD)))

    vec = np.concatenate([columns(first(n)) for n in ("ln_g", "ln_b", "hyp_b1", "hyp_b2", "sty_b1", "sty_b2")]
                         + [columns(second(n)) for n in ("b_ada", "bq", "bk", "b1", "g2", "beta2")]
                         + [columns(freq), columns(np.arange(P, dtype=np.float32))], axis=1).astype(np.float32)

    arrays = {
        "x": given["x"].reshape(B * T, D),
        "subject": given["itok_B_6_14"].reshape(B, 1).view(np.uint32),
        "timestep": given["itok_B_34_63"],
        "bias": given["fside_Bx16xSxS_0"],
        "mask": given["mask_Bx1xSxS_bk0"].reshape(B, T, T).view(np.uint32),
        "vec": vec, "const": const,
        "subj_emb": first("subj_emb"), "hyp_w1": first("hyp_w1"), "hyp_w2": first("hyp_w2"),
        "sty_w1": first("sty_w1"), "sty_w2": first("sty_w2"),
        "ada_w": chunks(second("W_ada")), "router": chunks(first("router_w")),
        "w1": first("exp_w1").reshape(E, C, P, FF).transpose(2, 0, 1, 3).reshape(P, E, C * FF),
        "w2": first("exp_w2").reshape(E, F, P, D).transpose(2, 0, 1, 3).reshape(P, E, F * D),
        "b1": first("exp_b1"), "b2": first("exp_b2"),
        "wq": chunks(second("Wq")), "wk": chunks(second("Wk")), "wv": chunks(second("Wv")), "wo": chunks(second("Wo")),
        "ff_w1": chunks(second("W1")), "ff_w2": chunks(second("W2")),
        "rows": np.stack([second("bv"), second("bo"), second("b2")]),
    }
    arrays = {k: np.ascontiguousarray(v) for k, v in arrays.items()}

    nc = bacc.Bacc("TRN2", target_bir_lowering=False, num_devices=1)
    io = {k: nc.dram_tensor(k + "_dram", v.shape, mybir.dt.from_np(v.dtype), kind="ExternalInput").ap() for k, v in arrays.items()}
    io["out"] = nc.dram_tensor("out_dram", (B * T, D), F32, kind="ExternalOutput").ap()
    layers(nc, io)
    result = run_bass_kernel_spmd(nc, [{k + "_dram": v for k, v in arrays.items()}], core_ids=[0])
    return result.results[0]["out_dram"].reshape(B, T, D)
```
